# Optimizing a Trainium2 kernel written in Bass

```python
import numpy as np
import jax
import jax.numpy as jnp

def _softmax(x, axis=-1):
    return jax.nn.softmax(x, axis=axis)

def _gelu(x):
    return jax.nn.gelu(x, approximate=True)

def _silu(x):
    return jax.nn.silu(x)

def _sigmoid(x):
    return jax.nn.sigmoid(x)

def _layernorm(x, axis=-1, eps=1e-05):
    m = jnp.mean(x, axis=axis, keepdims=True)
    v = jnp.var(x, axis=axis, keepdims=True)
    return (x - m) / jnp.sqrt(v + eps)

def _scatter_add(tgt, idx, src, axis=0):
    return tgt.at[idx].add(src)

def _segment_sum(src, seg, n):
    return jax.ops.segment_sum(src, seg, n)
kernel_name = 'mk_recurrent_d1_jaxref_r8_1aa4d4'

def setup_inputs(seed: int=0):
    np.random.seed(seed)
    _w = jnp.asarray

    def _L0_attn_setup():
        import jax, jax.numpy as jnp
        import numpy as np
        DIM = 128
        DIM_HEADS = 128
        HEADS = 8
        DHEAD = DIM_HEADS // HEADS
        EPS = 1e-06

        def _l2norm(t, axis=-1):
            n = jnp.sqrt(jnp.sum(t * t, axis=axis, keepdims=True))
            return t / jnp.maximum(n, 1e-12)
        key = jax.random.key(seed)
        k1, k2, k3 = jax.random.split(key, 3)
        x = jax.random.normal(k1, (8, 512, DIM), dtype=jnp.float32)
        norm_weight = jnp.ones((DIM,), dtype=jnp.float32)
        w_qkv = jax.random.normal(k2, (3 * DIM_HEADS, DIM), dtype=jnp.float32) * (1.0 / np.sqrt(DIM))
        temperature = jnp.zeros((HEADS, 1, 1), dtype=jnp.float32)
        w_out = jax.random.normal(k3, (DIM, DIM_HEADS), dtype=jnp.float32) * (1.0 / np.sqrt(DIM_HEADS))
        return {'x': x, 'norm_weight': norm_weight, 'w_qkv': w_qkv, 'temperature': temperature, 'w_out': w_out}
    _L0_attn_in = _L0_attn_setup()

    def _L0_ffn_setup():
        import jax, jax.numpy as jnp
        import numpy as np
        B, S, D, E, F = (2, 256, 128, 8, 512)
        key = jax.random.key(seed)
        ks = jax.random.split(key, 4)
        return {'hidden_states': jax.random.normal(ks[0], (B, S, D), dtype=jnp.float32), 'Wr': jax.random.normal(ks[1], (D, E), dtype=jnp.float32) * (1.0 / np.sqrt(D)), 'W1': jax.random.normal(ks[2], (E, D, F), dtype=jnp.float32) * (1.0 / np.sqrt(D)), 'b1': jnp.zeros((E, F), dtype=jnp.float32), 'W2': jax.random.normal(ks[3], (E, F, D), dtype=jnp.float32) * (1.0 / np.sqrt(F)), 'b2': jnp.zeros((E, D), dtype=jnp.float32)}
    _L0_ffn_in = _L0_ffn_setup()
    _d = {'L0_attn_x': _L0_attn_in['x'], 'L0_attn_norm_weight': _L0_attn_in['norm_weight'], 'L0_attn_w_qkv': _L0_attn_in['w_qkv'], 'L0_attn_temperature': _L0_attn_in['temperature'], 'L0_attn_w_out': _L0_attn_in['w_out'], 'L0_ffn_Wr': _L0_ffn_in['Wr'], 'L0_ffn_W1': _L0_ffn_in['W1'], 'L0_ffn_b1': _L0_ffn_in['b1'], 'L0_ffn_W2': _L0_ffn_in['W2'], 'L0_ffn_b2': _L0_ffn_in['b2']}
    _x0 = _d['L0_attn_x']
    _d['L0_attn_x'] = jax.random.normal(jax.random.fold_in(jax.random.key(seed), 1), (2, 1024, 128), dtype=_x0.dtype)
    del _x0
    return _d

def reference(L0_attn_x, L0_attn_norm_weight, L0_attn_w_qkv, L0_attn_temperature, L0_attn_w_out, L0_ffn_Wr, L0_ffn_W1, L0_ffn_b1, L0_ffn_W2, L0_ffn_b2):

    def _L0_attn_ref(x, norm_weight, w_qkv, temperature, w_out):
        import jax, jax.numpy as jnp
        import numpy as np
        DIM = 128
        DIM_HEADS = 128
        HEADS = 8
        DHEAD = DIM_HEADS // HEADS
        EPS = 1e-06

        def _l2norm(t, axis=-1):
            n = jnp.sqrt(jnp.sum(t * t, axis=axis, keepdims=True))
            return t / jnp.maximum(n, 1e-12)
        b, n, _ = x.shape
        ms = jnp.mean(x * x, axis=-1, keepdims=True)
        xn = x * jax.lax.rsqrt(ms + EPS) * norm_weight
        qkv = jnp.einsum('bnc,oc->bno', xn, w_qkv)
        qkv = qkv.reshape(b, n, 3, HEADS, DHEAD).transpose(2, 0, 3, 4, 1)
        q, k, v = (qkv[0], qkv[1], qkv[2])
        q = _l2norm(q)
        k = _l2norm(k)
        q = q * jnp.exp(temperature)
        sim = jnp.einsum('bhin,bhjn->bhij', q, k)
        attn = jax.nn.softmax(sim, axis=-1)
        out = jnp.einsum('bhij,bhjn->bhin', attn, v)
        out = out.transpose(0, 3, 1, 2).reshape(b, n, HEADS * DHEAD)
        return jnp.einsum('bnc,oc->bno', out, w_out)

    def _L0_ffn_ref(hidden_states, Wr, W1, b1, W2, b2):
        import jax, jax.numpy as jnp
        import numpy as np
        B, S, D, E, F = (2, 256, 128, 8, 512)
        b, s, d = hidden_states.shape
        e = Wr.shape[1]
        x = hidden_states.reshape(b * s, d)
        router_logits = x @ Wr
        router_probs = jax.nn.softmax(router_logits, axis=-1)
        expert_idx = jnp.argmax(router_probs, axis=-1)
        p_max = jnp.max(router_probs, axis=-1, keepdims=True)

        def expert_mlp(w1, bb1, w2, bb2):
            h = jax.nn.gelu(x @ w1 + bb1, approximate=False)
            return h @ w2 + bb2
        outs = jax.vmap(expert_mlp)(W1, b1, W2, b2)
        onehot = jax.nn.one_hot(expert_idx, e, dtype=x.dtype)
        next_states = jnp.einsum('te,etd->td', onehot, outs)
        out = p_max * next_states
        return out.reshape(b, s, d)
    x = L0_attn_x
    xn = _layernorm(x, axis=-1)
    s = _L0_attn_ref(xn, L0_attn_norm_weight, L0_attn_w_qkv, L0_attn_temperature, L0_attn_w_out)
    g = _silu(_L0_ffn_ref(xn, L0_ffn_Wr, L0_ffn_W1, L0_ffn_b1, L0_ffn_W2, L0_ffn_b2))
    x = x + s * g
    return x

_drawn_inputs = setup_inputs


def setup_inputs(seed=0):
    import zlib

    import numpy as np

    out = dict(_drawn_inputs(seed))
    spreads = {'L0_attn_norm_weight': (1.0, 0.6),
     'L0_attn_temperature': (0.0, 2.0),
     'L0_ffn_b1': (0.0, 0.8),
     'L0_ffn_b2': (0.0, 0.8)}
    factors = {}
    for name, (base, spread) in spreads.items():
        noise = np.random.default_rng([zlib.crc32(name.encode()), seed]).standard_normal(out[name].shape)
        drawn = base * np.exp(spread * noise) if base else spread * noise
        out[name] = jnp.asarray(drawn.astype(out[name].dtype))
    for name, factor in factors.items():
        out[name] = (out[name] * factor).astype(out[name].dtype)
    return out
```

```python
from contextlib import ExitStack

import concourse.bass as bass
from concourse import mybir

F32 = mybir.dt.float32
BF16 = mybir.dt.bfloat16
I32 = mybir.dt.int32
ALU = mybir.AluOpType
ACT = mybir.ActivationFunctionType
AX_X = mybir.AxisListType.X
At = bass.IndirectOffsetOnAxis

P = 128
NB = 2
NJ = 16
JB = NJ // NB
T = P * NJ
E = 8
F = 512
FC = F // P
NT = T // P + E - 1
DH = 16
SHIFT = 7

MEAN, RSTD, RA, RB, HALF_P = P, P + 1, P + 2, P + 3, P + 4
ROW = P + 8

LN_EPS = 1e-5
RMS_EPS = 1e-6
NORM_FLOOR = 1e-12
OUTSIDE = -1e30
NOWHERE = 4 * T


def build(nc, x, norm_w, w_qkv, temperature, w_out, w_r, w1, b1, w2, b2, out):
    x_v = x.rearrange("b (p j) d -> b p j d", p=P)
    out_v = out.rearrange("b n d -> (b n) d")
    rows = nc.dram_tensor("token_rows", (T, ROW), F32).ap()
    rows_v = rows.rearrange("(b p j) r -> b p j r", b=NB, p=P)

    with ExitStack() as ctx:
        def sb(name, shape, dt=F32):
            return ctx.enter_context(nc.sbuf_tensor(name, shape, dt))

        def bank(name):
            return ctx.enter_context(nc.psum_tensor(name, [P, 512], F32))

        def sem(name):
            return ctx.enter_context(nc.semaphore(name))

        ident = sb("ident", [P, P])
        ones = sb("ones", [P, P])
        ones_bf = sb("ones_bf", [P, P], BF16)
        before = sb("before", [P, P], BF16)
        head_gap = sb("head_gap", [P, P])
        head_rows = sb("head_rows", [E, P])
        slot_iota = sb("slot_iota", [P, P], BF16)
        tile_iota = sb("tile_iota", [P, NT])
        tile_start = sb("tile_start", [1, NT])
        rev_e = sb("rev_e", [P, E])
        earlier_e = sb("earlier_e", [P, E, E])
        id_p = sb("id_p", [P, 1])
        id_j = sb("id_j", [P, NJ])
        xe = sb("xe", [P, NJ, ROW])
        wqkv = sb("wqkv", [P, 3, P])
        wout = sb("wout", [P, P])
        nw = sb("nw", [P, 1])
        temp = sb("temp", [E, 1])
        wr = sb("wr", [P, E])
        w1s = sb("w1s", [P, E * F])
        w2s = sb("w2s", [P, E * F])
        bs = sb("bs", [P, E, F + P])
        stats = sb("stats", [P, NJ, 6])
        v12 = sb("v12", [P, 2, NJ])
        rs = sb("rs", [P, 2, NJ])
        rt = sb("rt", [P, 2, NJ])
        xn = sb("xn", [P, NJ, P])
        xr = sb("xr", [P, NJ, P])
        xnT = sb("xnT", [P, NJ * P])
        lmax = sb("lmax", [P, NJ])
        is_max = sb("is_max", [P, NJ, E])
        best = sb("best", [P, NJ])
        chosen = sb("chosen", [P, NJ + 1, E], BF16)
        below = sb("below", [P, NJ, E])
        expo = sb("expo", [P, NJ, E])
        psum_e = sb("psum_e", [P, NJ])
        half_p = sb("half_p", [P, NJ])
        rfac = sb("rfac", [P, NJ])
        tiles_i = sb("tiles_i", [P, 2, E], I32)
        tiles_f = sb("tiles_f", [P, E])
        ee = sb("ee", [P, E, E])
        base = sb("base", [P, E])
        place = sb("place", [P, NJ, E])
        pos = sb("pos", [P, NJ])
        pos_i = sb("pos_i", [P, NJ], I32)
        ab_i = sb("ab_i", [P, 2, NJ], I32)
        ab = sb("ab", [P, 2, NJ])
        in_tile = sb("in_tile", [P, NJ, NT], BF16)
        tagged = sb("tagged", [P, NJ, 2, NT], BF16)
        in_slot = sb("in_slot", [P, NJ, P], BF16)
        late = sb("late", [P, NT])
        token1 = sb("token1", [P, NT])
        from_row = sb("from_row", [P, NT], I32)
        to_row = sb("to_row", [P, NT], I32)
        et = sb("et", [1, NT, E - 1])
        ef = sb("ef", [1, NT])
        w_at = sb("w_at", [1, NT], I32)
        b_at = sb("b_at", [1, NT], I32)
        wqkT = sb("wqkT", [P, 2 * P])
        woutT = sb("woutT", [P, P])
        gram = sb("gram", [P, NB, P])
        gw = sb("gw", [P, NB, 2 * P])
        prod = sb("prod", [P, NB, 2 * P])
        n2 = sb("n2", [P, 4])
        nr = sb("nr", [P, 4])
        ni = sb("ni", [P, 4])
        nt_ = sb("nt_", [P, 4])
        etemp = sb("etemp", [P, 1])
        qscale = sb("qscale", [P, NB])
        kdiag = sb("kdiag", [P, NB, P])
        sim = sb("sim", [P, NB, P])
        simq = sb("simq", [P, NB, P])
        smax = sb("smax", [P, NB])
        prob = sb("prob", [P, NB, P])
        psumA = sb("psumA", [P, NB])
        pinv = sb("pinv", [P, NB])
        att = sb("att", [P, NB, P])
        mid = sb("mid", [P, NB, P])
        mat = sb("mat", [P, NB * P])
        xg = sb("xg", [P, NT, ROW])
        sg = sb("sg", [P, NT, P])
        xns = [sb(f"xns{i}", [P, P]) for i in range(2)]
        xTs = [sb(f"xTs{i}", [P, P]) for i in range(2)]
        hs = [sb(f"hs{i}", [P, F]) for i in range(2)]
        gs = [sb(f"gs{i}", [P, F]) for i in range(2)]
        zs = [sb(f"zs{i}", [P, P]) for i in range(2)]
        th = [sb(f"th{i}", [P, P]) for i in range(2)]
        qs = sb("qs", [P, P])
        us = sb("us", [P, P])

        banks = [bank(f"bank{i}") for i in range(8)]
        h_ps, hT_ps, xT_ps, y_ps, s_ps = banks[0:2], banks[2:4], banks[4], banks[5], banks[6]
        logits_ps = banks[4][:, 0:NJ * E].rearrange("p (j e) -> p j e", e=E)
        rank_ps = banks[5][:, 0:(NJ + 1) * E].rearrange("p (j e) -> p j e", e=E)
        slots_ps = banks[6][:, 0:2 * NT].rearrange("p (g t) -> p g t", g=2)
        wT_ps = banks[7]
        gram_ps = banks[7][:, 0:NB * P].rearrange("p (b c) -> p b c", b=NB)
        gw_ps = banks[0][:, :].rearrange("p (b c) -> p b c", b=NB)
        sim_ps = banks[1][:, 0:NB * P].rearrange("p (b c) -> p b c", b=NB)
        norm_ps = banks[2][:, 0:4]
        krow_ps = banks[3][:, 0:NB * P].rearrange("p (b c) -> p b c", b=NB)
        temp_ps = banks[2][:, 8:9]
        mid_ps = banks[2][:, 0:NB * P].rearrange("p (b c) -> p b c", b=NB)
        mat_ps = banks[3][:, 0:NB * P].rearrange("p (b c) -> p b c", b=NB)

        x_in = [sem(f"x_in{b}") for b in range(NB)]
        att_w_in = sem("att_w_in")
        wr_in = sem("wr_in")
        w1_in, w2_in, b1_in, b2_in = sem("w1_in"), sem("w2_in"), sem("b1_in"), sem("b2_in")
        rows_out = sem("rows_out")
        row_in = [sem(f"row_in{i}") for i in range(2)]
        result_out = sem("result_out")
        pool_step, dve_step = sem("pool_step"), sem("dve_step")
        const_ready = sem("const_ready")
        var_ready, root_ready, rs_ready = sem("var_ready"), sem("root_ready"), sem("rs_ready")
        xn_tok, xr_tok, xT_tok_ps, xT_tok = sem("xn_tok"), sem("xr_tok"), sem("xT_tok_ps"), sem("xT_tok")
        logits_done, below_ready, expo_ready = sem("logits_done"), sem("below_ready"), sem("expo_ready")
        chosen_ready, rank_done, tags_ready = sem("chosen_ready"), sem("rank_done"), sem("tags_ready")
        in_slot_ready, slots_done = sem("in_slot_ready"), sem("slots_done")
        scalars_ready, from_ready, to_ready, tables_ready = (
            sem("scalars_ready"), sem("from_ready"), sem("to_ready"), sem("tables_ready"))
        wT_done, wT_ready, temp_done = sem("wT_done"), sem("wT_ready"), sem("temp_done")
        gram_done, gram_ready, gw_done, gw_ready = sem("gram_done"), sem("gram_ready"), sem("gw_done"), sem("gw_ready")
        prod_ready, norm_done, n2_ready, nroot_ready = sem("prod_ready"), sem("norm_done"), sem("n2_ready"), sem("nroot_ready")
        etemp_ready, kdiag_ready, krow_done = sem("etemp_ready"), sem("kdiag_ready"), sem("krow_done")
        sim_ready, prob_ready, att_ready = sem("sim_ready"), sem("prob_ready"), sem("att_ready")
        mid_done, mid_ready, mat_done, mat_ready = sem("mid_done"), sem("mid_ready"), sem("mat_done"), sem("mat_ready")
        xn_ready, xT_done, xT_ready = sem("xn_ready"), sem("xT_done"), sem("xT_ready")
        h_done, h_ready, hT_done, gelu_ready = sem("h_done"), sem("h_ready"), sem("hT_done"), sem("gelu_ready")
        s_done, s0_ready, s_ready = sem("s_done"), sem("s0_ready"), sem("s_ready")
        y_done, z_ready, tanh_ready = sem("y_done"), sem("z_ready"), sem("tanh_ready")
        q_done, u_done, o_ready = sem("q_done"), sem("u_done"), sem("o_ready")

        def need(eng, semaphore, value):
            if not isinstance(value, int) or value > 0:
                eng.wait_ge(semaphore, value)

        biases = bs[:].rearrange("p e f -> p (e f)")

        def offsets(engine, table, most):
            return nc.values_load_multi_w_load_instructions(
                table[0:1, :], engines=[engine], min_val=0, max_val=most, 
                skip_runtime_bounds_check_because="an expert is 0 to 7 by its construction")[1]

        block = ctx.enter_context(nc.Block())

        @block.sync
        def _(sp):
            for b in range(NB):
                sp.dma_start(xe[:, b * JB:(b + 1) * JB, 0:P], x_v[b]).then_inc(x_in[b], 16)
            sp.dma_start(wr[:], w_r).then_inc(wr_in, 16)
            sp.dma_start(wqkv[:], w_qkv.rearrange("(s o) c -> o s c", s=3)).then_inc(att_w_in, 16)
            sp.dma_start(wout[:], w_out).then_inc(att_w_in, 16)
            sp.dma_start(nw[:], norm_w.rearrange("(c a) -> c a", a=1)).then_inc(att_w_in, 16)
            sp.dma_start(temp[:], temperature.rearrange("h a b -> h (a b)")).then_inc(att_w_in, 16)
            sp.dma_start(w1s[:].rearrange("d (e f) -> d e f", e=E), w1.rearrange("e d f -> d e f")).then_inc(w1_in, 16)
            sp.dma_start(bs[:, :, 0:F], b1.partition_broadcast(P)).then_inc(b1_in, 16)
            sp.dma_start(w2s[:].rearrange("f (e c d) -> f e c d", e=E, c=FC),
                         w2.rearrange("e (c f) d -> f e c d", c=FC)).then_inc(w2_in, 16)
            sp.dma_start(bs[:, :, F:F + P], b2.partition_broadcast(P)).then_inc(b2_in, 16)
            sp.wait_ge(scalars_ready, 1)
            for b in range(NB):
                sp.dma_start(rows_v[b], xe[:, b * JB:(b + 1) * JB, :]).then_inc(rows_out, 16)

        @block.gpsimd
        def _(pool):
            steps = [0]

            def link(ins):
                steps[0] += 1
                ins.then_inc(pool_step, 1)
                pool.wait_ge(pool_step, steps[0])

            g = nc.gpsimd
            link(g.memset(ones[:], 1.0))
            link(g.affine_select(out=ident[:], in_=ones[:], compare_op=ALU.is_equal, fill=0.0, base=0,
                                 pattern=[[-1, P]], channel_multiplier=1))
            g.memset(ones_bf[:], 1.0)
            g.memset(xe[:, :, MEAN:ROW], 0.0)
            g.memset(chosen[:, NJ:NJ + 1, :], 0.0)
            g.affine_select(out=before[:], in_=ones[:], compare_op=ALU.is_gt, fill=0.0, base=0,
                            pattern=[[1, P]], channel_multiplier=-1)
            g.iota(slot_iota[:], [[1, P]], base=0, channel_multiplier=0, allow_small_or_imprecise_dtypes=True)
            g.iota(tile_iota[:], [[1, NT]], base=0, channel_multiplier=0, allow_small_or_imprecise_dtypes=True)
            g.iota(tile_start[:], [[P, NT]], base=0, channel_multiplier=0, allow_small_or_imprecise_dtypes=True)
            g.iota(rev_e[:], [[-1, E]], base=E, channel_multiplier=0, allow_small_or_imprecise_dtypes=True)
            g.iota(id_p[:], [[0, 1]], base=0, channel_multiplier=JB, allow_small_or_imprecise_dtypes=True)
            g.iota(id_j[:], [[P, NB], [1, JB]], base=1, channel_multiplier=0, allow_small_or_imprecise_dtypes=True)
            link(g.memset(earlier_e[:], float(P)))
            g.affine_select(out=earlier_e[:], in_=earlier_e[:], compare_op=ALU.is_gt, fill=0.0, base=0,
                            pattern=[[1, E], [-1, E]], channel_multiplier=0)
            link(g.memset(head_gap[:], 0.0))
            gap = head_gap[:].rearrange("p (h i) -> p h i", i=DH)
            link(g.affine_select(out=gap, in_=gap, compare_op=ALU.is_ge, fill=OUTSIDE, base=0,
                                 pattern=[[-DH, E], [0, DH]], channel_multiplier=1))
            link(g.affine_select(out=gap, in_=gap, compare_op=ALU.is_ge, fill=OUTSIDE, base=DH - 1,
                                 pattern=[[DH, E], [0, DH]], channel_multiplier=-1))
            hr = head_rows[:].rearrange("p (h i) -> p h i", i=DH)
            g.affine_select(out=hr, in_=ones[0:E, :].rearrange("p (h i) -> p h i", i=DH), compare_op=ALU.is_equal,
                            fill=0.0, base=0, pattern=[[-1, E], [0, DH]], channel_multiplier=1
                            ).then_inc(const_ready, 1)

            pool.wait_ge(rs_ready, 1)
            for j in range(NJ):
                g.tensor_scalar(xr[:, j, :], xe[:, j, 0:P], xe[:, j, MEAN:MEAN + 1], rs[:, 1, j:j + 1],
                                ALU.subtract, ALU.mult).then_inc(xr_tok, 1)

            for b in range(NB):
                pool.wait_ge(gw_ready, 1)
                g.tensor_tensor(prod[:, b, :], gw[:, b, :], wqkT[:], ALU.mult).then_inc(prod_ready, 1)

            pool.wait_ge(rows_out, 16 * NB)
            pool.wait_ge(from_ready, 1)
            for k in range(NT):
                if k >= 2:
                    pool.wait_ge(row_in[k % 2], 16 * (k // 2))
                g.indirect_dma_start(xg[:, k, :], None, rows, At(ap=from_row[:, k:k + 1], axis=0)
                                     ).then_inc(row_in[k % 2], 16)
            pool.wait_ge(to_ready, 1)
            for k in range(NT):
                pool.wait_ge(o_ready, k + 1)
                g.indirect_dma_start(out_v, At(ap=to_row[:, k:k + 1], axis=0), xg[:, k, 0:P], None,
                                     bounds_check=T - 1, oob_is_err=False).then_inc(result_out, 16)
            pool.wait_ge(result_out, 16 * NT)

        @block.vector
        def _(dve):
            v = nc.vector
            steps = [0]

            def link(ins):
                steps[0] += 1
                ins.then_inc(dve_step, 1)
                dve.wait_ge(dve_step, steps[0])

            dve.wait_ge(const_ready, 1)
            for j in range(NJ):
                if j % JB == 0:
                    dve.wait_ge(x_in[j // JB], 16)
                last = v.bn_stats(stats[:, j, :], xe[:, j, 0:P])
            link(last)
            for j in range(NJ):
                last = v.bn_aggr(xe[:, j, MEAN:MEAN + 2], stats[:, j, :])
            link(last)
            var = xe[:, :, MEAN + 1]
            v.tensor_scalar(v12[:, 0, :], var, LN_EPS, None, ALU.add)
            v.tensor_scalar(v12[:, 1, :], var, 1.0 + RMS_EPS, RMS_EPS * LN_EPS, ALU.mult, ALU.add
                            ).then_inc(var_ready, 1)
            dve.wait_ge(var_ready, 1)
            dve.wait_ge(root_ready, 1)
            link(v.reciprocal(rs[:], rs[:]))
            link(v.tensor_tensor(rt[:], rs[:], rs[:], ALU.mult))
            link(v.tensor_tensor(rt[:], rt[:], v12[:], ALU.mult))
            link(v.tensor_scalar(rt[:], rt[:], -0.5, 1.5, ALU.mult, ALU.add))
            v.tensor_tensor(rs[:], rs[:], rt[:], ALU.mult).then_inc(rs_ready, 1)
            dve.wait_ge(rs_ready, 1)
            v.tensor_copy(xe[:, :, RSTD], rs[:, 0, :])
            for j in range(NJ):
                v.tensor_scalar(xn[:, j, :], xe[:, j, 0:P], xe[:, j, MEAN:MEAN + 1], rs[:, 0, j:j + 1],
                                ALU.subtract, ALU.mult).then_inc(xn_tok, 1)
            link(v.tensor_tensor(rfac[:], rs[:, 0, :], v12[:, 0, :], ALU.mult))
            link(v.tensor_tensor(rfac[:], rfac[:], rs[:, 1, :], ALU.mult))

            dve.wait_ge(logits_done, 1)
            link(v.tensor_reduce(lmax[:], logits_ps, AX_X, ALU.max))
            link(v.tensor_tensor(is_max[:], logits_ps, lmax[:].unsqueeze(2).to_broadcast([P, NJ, E]), ALU.is_equal))
            v.tensor_tensor(below[:], logits_ps, lmax[:].unsqueeze(2).to_broadcast([P, NJ, E]), ALU.subtract
                            ).then_inc(below_ready, 1)
            rev = rev_e[:].unsqueeze(1).to_broadcast([P, NJ, E])
            link(v.tensor_tensor(is_max[:], is_max[:], rev, ALU.mult))
            link(v.tensor_reduce(best[:], is_max[:], AX_X, ALU.max))
            v.tensor_tensor(chosen[:, 0:NJ, :], rev, best[:].unsqueeze(2).to_broadcast([P, NJ, E]), ALU.is_equal
                            ).then_inc(chosen_ready, 1)

            dve.wait_ge(expo_ready, 1)
            link(v.tensor_reduce(psum_e[:], expo[:], AX_X, ALU.add))
            link(v.tensor_scalar(psum_e[:], psum_e[:], 2.0, None, ALU.mult))
            link(v.reciprocal(half_p[:], psum_e[:]))
            v.tensor_copy(xe[:, :, HALF_P], half_p[:])
            v.tensor_tensor(xe[:, 0:JB, RA], rfac[:, 0:JB], half_p[:, 0:JB], ALU.mult)
            v.tensor_tensor(xe[:, JB:NJ, RB], rfac[:, JB:NJ], half_p[:, JB:NJ], ALU.mult
                            ).then_inc(scalars_ready, 1)

            dve.wait_ge(rank_done, 1)
            dve.wait_ge(chosen_ready, 1)
            link(v.tensor_scalar(tiles_i[:, 0, :], rank_ps[:, NJ, :], float(P - 1), None, ALU.add))
            link(v.tensor_scalar(tiles_i[:, 1, :], tiles_i[:, 0, :], SHIFT, None, ALU.arith_shift_right))
            link(v.tensor_copy(tiles_f[:], tiles_i[:, 1, :]))
            link(v.tensor_tensor(ee[:], earlier_e[:], tiles_f[:].unsqueeze(1).to_broadcast([P, E, E]), ALU.mult))
            link(v.tensor_reduce(base[:], ee[:], AX_X, ALU.add))
            link(v.tensor_tensor(place[:], rank_ps[:, 0:NJ, :], base[:].unsqueeze(1).to_broadcast([P, NJ, E]), ALU.add))
            link(v.tensor_tensor(place[:], place[:], chosen[:, 0:NJ, :], ALU.mult))
            link(v.tensor_reduce(pos[:], place[:], AX_X, ALU.add))
            link(v.tensor_copy(pos_i[:], pos[:]))
            v.tensor_scalar(ab_i[:, 0, :], pos_i[:], SHIFT, None, ALU.arith_shift_right)
            link(v.tensor_scalar(ab_i[:, 1, :], pos_i[:], P - 1, None, ALU.bitwise_and))
            link(v.tensor_copy(ab[:], ab_i[:]))
            link(v.tensor_tensor(in_tile[:], ab[:, 0, :].unsqueeze(2).to_broadcast([P, NJ, NT]),
                                 tile_iota[:].unsqueeze(1).to_broadcast([P, NJ, NT]), ALU.is_equal))
            v.tensor_scalar(tagged[:, :, 0, :], in_tile[:], id_p[:, 0:1], None, ALU.mult)
            v.tensor_tensor(tagged[:, :, 1, :], in_tile[:], id_j[:].unsqueeze(2).to_broadcast([P, NJ, NT]), ALU.mult
                            ).then_inc(tags_ready, 1)
            for j in range(NJ):
                v.tensor_scalar(in_slot[:, j, :], slot_iota[:], ab[:, 1, j:j + 1], None, ALU.is_equal
                                ).then_inc(in_slot_ready, 1)
            dve.wait_ge(slots_done, 1)
            link(v.tensor_scalar(late[:], slots_ps[:, 1, :], float(P), float(T // NB - P), ALU.is_ge, ALU.mult))
            link(v.tensor_tensor(late[:], late[:], slots_ps[:, 1, :], ALU.add))
            link(v.tensor_tensor(token1[:], late[:], slots_ps[:, 0, :], ALU.add))
            v.tensor_scalar(from_row[:], token1[:], -1.0, 0.0, ALU.add, ALU.max).then_inc(from_ready, 1)
            link(v.tensor_tensor(et[:], base[0:1, 1:E].unsqueeze(1).to_broadcast([1, NT, E - 1]),
                                 tile_start[:].unsqueeze(2).to_broadcast([1, NT, E - 1]), ALU.is_le))
            link(v.tensor_reduce(ef[:], et[:], AX_X, ALU.add))
            v.tensor_scalar(w_at[:], ef[:], float(F), None, ALU.mult)
            v.tensor_scalar(b_at[:], ef[:], float(F + P), None, ALU.mult).then_inc(tables_ready, 1)
            link(v.tensor_scalar(late[:], token1[:], 0.0, float(NOWHERE), ALU.is_equal, ALU.mult))
            link(v.tensor_tensor(token1[:], late[:], token1[:], ALU.add))
            v.tensor_scalar(to_row[:], token1[:], -1.0, None, ALU.add).then_inc(to_ready, 1)

            dve.wait_ge(norm_done, 1)
            v.tensor_scalar(n2[:], norm_ps, 0.0, None, ALU.max).then_inc(n2_ready, 1)
            dve.wait_ge(n2_ready, 1)
            dve.wait_ge(nroot_ready, 1)
            link(v.tensor_scalar(nr[:], nr[:], NORM_FLOOR, None, ALU.max))
            link(v.reciprocal(ni[:], nr[:]))
            link(v.tensor_tensor(nt_[:], n2[:], ni[:], ALU.mult))
            link(v.tensor_tensor(nt_[:], nt_[:], nr[:], ALU.add))
            link(v.tensor_scalar(nt_[:], nt_[:], 0.5, NORM_FLOOR, ALU.mult, ALU.max))
            link(v.reciprocal(ni[:], nt_[:]))
            dve.wait_ge(etemp_ready, 1)
            v.tensor_scalar(qscale[:], ni[:, 0:NB], etemp[:, 0:1], None, ALU.mult)
            for b in range(NB):
                last = v.tensor_scalar(kdiag[:, b, :], ident[:], ni[:, NB + b:NB + b + 1], None, ALU.mult)
            last.then_inc(kdiag_ready, 1)
            dve.wait_ge(kdiag_ready, 1)
            for b in range(NB):
                last = v.tensor_scalar(simq[:, b, :], sim_ps[:, b, :], qscale[:, b:b + 1], None, ALU.mult)
            link(last)
            dve.wait_ge(krow_done, 1)
            link(v.tensor_tensor(sim[:], simq[:], krow_ps, ALU.mult))
            link(v.tensor_tensor(sim[:], sim[:], head_gap[:].unsqueeze(1).to_broadcast([P, NB, P]), ALU.add))
            link(v.tensor_reduce(smax[:], sim[:], AX_X, ALU.max))
            v.tensor_scalar(smax[:], smax[:], -1.0, None, ALU.mult).then_inc(sim_ready, 1)
            dve.wait_ge(prob_ready, 1)
            link(v.reciprocal(pinv[:], psumA[:]))
            for b in range(NB):
                last = v.tensor_scalar(att[:, b, :], prob[:, b, :], pinv[:, b:b + 1], None, ALU.mult)
            last.then_inc(att_ready, 1)

            def normalise(k, odd):
                dve.wait_ge(row_in[odd], 8 * (k + 1) if odd else 8 * k + 16)
                need(dve, xT_done, k - 1)
                row = xg[:, bass.ds(k, 1), :].rearrange("p a r -> p (a r)")
                v.tensor_scalar(xns[odd][:], row[:, 0:P], row[:, MEAN:MEAN + 1], row[:, RSTD:RSTD + 1],
                                ALU.subtract, ALU.mult).then_inc(xn_ready, 1)

            def hidden(k, odd):
                dve.wait_ge(h_done, k + 1)
                need(dve, hT_done, k - 1)
                v.tensor_tensor(hs[odd][:], h_ps[odd][:], biases[:, bass.ds(b_off[k], F)], ALU.add).then_inc(h_ready, 1)

            def attention(k):
                dve.wait_ge(s0_ready, k + 1)
                row = xg[:, bass.ds(k, 1), :].rearrange("p a r -> p (a r)")
                acc = sg[:, bass.ds(k, 1), :].rearrange("p a r -> p (a r)")
                v.scalar_tensor_tensor(out=acc, in0=s_ps[:, P:2 * P], scalar=row[:, RB:RB + 1], in1=acc,
                                       op0=ALU.mult, op1=ALU.add).then_inc(s_ready, 1)

            def ffn_out(k, odd):
                dve.wait_ge(y_done, k + 1)
                v.tensor_tensor(zs[odd][:], y_ps[:, 0:P], biases[:, bass.ds(b_off[k] + F, P)], ALU.add).then_inc(z_ready, 1)

            def gate(k, odd):
                dve.wait_ge(tanh_ready, k + 1)
                need(dve, u_done, k)
                v.scalar_tensor_tensor(out=qs[:], in0=th[odd][:], scalar=1.0, in1=zs[odd][:],
                                       op0=ALU.add, op1=ALU.mult).then_inc(q_done, 1)

            def times_attention(k):
                acc = sg[:, bass.ds(k, 1), :].rearrange("p a r -> p (a r)")
                dve.wait_ge(q_done, k + 1)
                dve.wait_ge(s_ready, k + 1)
                need(dve, o_ready, k)
                v.tensor_tensor(us[:], qs[:], acc, ALU.mult).then_inc(u_done, 1)

            def add_x(k):
                row = xg[:, bass.ds(k, 1), :].rearrange("p a r -> p (a r)")
                dve.wait_ge(u_done, k + 1)
                v.tensor_tensor(row[:, 0:P], us[:], row[:, 0:P], ALU.add).then_inc(o_ready, 1)

            def turn(i, odd, first=0, last=NT - 1):
                def on(k):
                    return not isinstance(i, int) or 0 <= k < NT
                if on(i + 1):
                    hidden(i + 1, 1 - odd)
                if on(i - 2):
                    gate(i - 2, odd)
                if on(i + 1):
                    attention(i + 1)
                if on(i + 3):
                    normalise(i + 3, 1 - odd)
                if on(i - 2):
                    times_attention(i - 2)
                if on(i - 1):
                    ffn_out(i - 1, 1 - odd)
                if on(i - 2):
                    add_x(i - 2)

            dve.wait_ge(b1_in, 16)
            dve.wait_ge(b2_in, 16)
            dve.wait_ge(tables_ready, 1)
            b_off = offsets(mybir.EngineType.DVE, b_at, (E - 1) * (F + P))
            for i in range(-4, NT + 2):
                turn(i, i % 2)

        @block.scalar
        def _(act):
            a = nc.scalar
            act.wait_ge(wT_done, 1)
            act.wait_ge(att_w_in, 64)
            a.activation(wqkT[:], wT_ps[:, 0:2 * P], ACT.Copy, scale=nw[:, 0:1])
            a.activation(woutT[:], wT_ps[:, 2 * P:3 * P], ACT.Copy).then_inc(wT_ready, 1)
            act.wait_ge(var_ready, 1)
            a.activation(rs[:], v12[:], ACT.Sqrt).then_inc(root_ready, 1)
            for g4 in range(4):
                act.wait_ge(xT_tok_ps, g4 + 1)
                a.activation(xnT[:, g4 * F:(g4 + 1) * F], banks[g4][:], ACT.Copy).then_inc(xT_tok, 1)
            act.wait_ge(below_ready, 1)
            a.activation(expo[:], below[:], ACT.Exp).then_inc(expo_ready, 1)
            act.wait_ge(temp_done, 1)
            a.activation(etemp[:], temp_ps, ACT.Exp).then_inc(etemp_ready, 1)
            act.wait_ge(gram_done, NB)
            a.activation(gram[:], gram_ps, ACT.Copy).then_inc(gram_ready, 1)
            act.wait_ge(gw_done, 1)
            a.activation(gw[:], gw_ps, ACT.Copy).then_inc(gw_ready, 1)
            act.wait_ge(n2_ready, 1)
            a.activation(nr[:], n2[:], ACT.Sqrt).then_inc(nroot_ready, 1)
            act.wait_ge(sim_ready, 1)
            for b in range(NB):
                last = a.activation(prob[:, b, :], sim[:, b, :], ACT.Exp, bias=smax[:, b:b + 1],
                                    accum_out=psumA[:, b:b + 1])
            last.then_inc(prob_ready, 1)
            act.wait_ge(mid_done, 1)
            a.activation(mid[:], mid_ps, ACT.Copy).then_inc(mid_ready, 1)
            act.wait_ge(mat_done, 1)
            a.activation(mat[:].rearrange("p (b c) -> p b c", b=NB), mat_ps, ACT.Copy, scale=nw[:, 0:1]
                         ).then_inc(mat_ready, 1)

            def keep_xT(k, odd):
                act.wait_ge(xT_done, k + 1)
                need(act, s_done, k - 1)
                a.activation(xTs[odd][:], xT_ps[:, 0:P], ACT.Copy).then_inc(xT_ready, 1)

            def attention(k):
                act.wait_ge(s_done, k + 1)
                a.activation(sg[:, bass.ds(k, 1), :].rearrange("p a r -> p (a r)"), s_ps[:, 0:P], ACT.Copy,
                             scale=xg[:, bass.ds(k, 1), RA:RA + 1].rearrange("p a r -> p (a r)")
                             ).then_inc(s0_ready, 1)

            def gelu(k, odd):
                act.wait_ge(hT_done, k + 1)
                need(act, y_done, k - 1)
                a.activation(gs[odd][:], hT_ps[odd][:], ACT.Gelu).then_inc(gelu_ready, 1)

            def tanh(k, odd):
                act.wait_ge(z_ready, k + 1)
                need(act, q_done, k - 1)
                a.activation(th[odd][:], zs[odd][:], ACT.Tanh,
                             scale=xg[:, bass.ds(k, 1), HALF_P:HALF_P + 1].rearrange("p a r -> p (a r)")
                             ).then_inc(tanh_ready, 1)

            def turn(i, odd):
                def on(k):
                    return not isinstance(i, int) or 0 <= k < NT
                if on(i + 2):
                    keep_xT(i + 2, odd)
                if on(i + 1):
                    attention(i + 1)
                if on(i):
                    gelu(i, odd)
                if on(i - 1):
                    tanh(i - 1, 1 - odd)

            for i in range(-2, NT + 1):
                turn(i, i % 2)

        @block.tensor
        def _(pe):
            t = nc.tensor
            pe.wait_ge(const_ready, 1)
            pe.wait_ge(att_w_in, 64)
            t.transpose(wT_ps[:, 0:P], wqkv[:, 0, :], ident[:])
            t.transpose(wT_ps[:, P:2 * P], wqkv[:, 1, :], ident[:])
            t.transpose(wT_ps[:, 2 * P:3 * P], wout[:], ident[:]).then_inc(wT_done, 1)
            for j in range(NJ):
                pe.wait_ge(xn_tok, j + 1)
                last = t.transpose(banks[j // 4][:, (j % 4) * P:(j % 4 + 1) * P], xn[:, j, :], ident[:])
                if j % 4 == 3:
                    last.then_inc(xT_tok_ps, 1)
            pe.wait_ge(wr_in, 16)
            for j in range(NJ):
                if j % 4 == 0:
                    pe.wait_ge(xT_tok, j // 4 + 1)
                last = t.matmul(logits_ps[:, j, :], xnT[:, j * P:(j + 1) * P], wr[:], start=True, stop=True)
            last.then_inc(logits_done, 1)
            t.matmul(temp_ps, head_rows[:], temp[:], start=True, stop=True).then_inc(temp_done, 1)

            def grams(b):
                for j in range(b * JB, (b + 1) * JB):
                    pe.wait_ge(xr_tok, j + 1)
                    last = t.matmul(gram_ps[:, b, :], xr[:, j, :], xr[:, j, :],
                                    start=(j == b * JB), stop=(j == (b + 1) * JB - 1))
                last.then_inc(gram_done, 1)

            pe.wait_ge(wT_ready, 1)
            grams(0)
            pe.wait_ge(chosen_ready, 1)
            t.matmul(rank_ps, before[:], chosen[:], start=True, stop=False, skip_group_check=True)
            for c in range(1, NJ + 1):
                last = t.matmul(rank_ps[:, c:, :], ones_bf[:], chosen[:, 0:NJ + 1 - c, :], start=False,
                                stop=(c == NJ), skip_group_check=True)
            last.then_inc(rank_done, 1)
            grams(1)
            pe.wait_ge(gram_ready, 1)
            for b in range(NB):
                last = t.matmul(gw_ps[:, b, :], gram[:, b, :], wqkT[:], start=True, stop=True)
            last.then_inc(gw_done, 1)
            pe.wait_ge(tags_ready, 1)
            for j in range(NJ):
                pe.wait_ge(in_slot_ready, j + 1)
                last = t.matmul(slots_ps, in_slot[:, j, :], tagged[:, j, :, :], start=(j == 0), stop=(j == NJ - 1))
            last.then_inc(slots_done, 1)
            pe.wait_ge(gw_ready, 1)
            for b in range(NB):
                t.matmul(sim_ps[:, b, :], wqkT[:, 0:P], gw[:, b, P:2 * P], start=True, stop=True)
            pe.wait_ge(prod_ready, NB)
            pe.wait_ge(etemp_ready, 1)
            for b in range(NB):
                for s in range(2):
                    last = t.matmul(norm_ps[:, s * NB + b:s * NB + b + 1], prod[:, b, s * P:(s + 1) * P],
                                    ones[:, 0:1], start=True, stop=True)
            last.then_inc(norm_done, 1)
            pe.wait_ge(kdiag_ready, 1)
            for b in range(NB):
                last = t.matmul(krow_ps[:, b, :], ones[:], kdiag[:, b, :], start=True, stop=True)
            last.then_inc(krow_done, 1)
            pe.wait_ge(att_ready, 1)
            for b in range(NB):
                last = t.matmul(mid_ps[:, b, :], att[:, b, :], woutT[:], start=True, stop=True)
            last.then_inc(mid_done, 1)
            pe.wait_ge(mid_ready, 1)
            for b in range(NB):
                last = t.matmul(mat_ps[:, b, :], wqkv[:, 2, :], mid[:, b, :], start=True, stop=True)
            last.then_inc(mat_done, 1)

            def transpose_x(k, odd):
                pe.wait_ge(xn_ready, k + 1)
                need(pe, xT_ready, k)
                t.transpose(xT_ps[:, 0:P], xns[odd][:], ident[:]).then_inc(xT_done, 1)

            def product1(k, odd):
                pe.wait_ge(xT_ready, k + 1)
                need(pe, h_ready, k - 1)
                t.matmul(h_ps[odd][:], xTs[odd][:], w1s[:, bass.ds(w_off[k], F)], start=True, stop=True
                         ).then_inc(h_done, 1)

            def attention(k, odd):
                need(pe, s_ready, k)
                t.matmul(s_ps[:, 0:NB * P], xTs[odd][:], mat[:], start=True, stop=True).then_inc(s_done, 1)

            def transpose_h(k, odd):
                pe.wait_ge(h_ready, k + 1)
                need(pe, gelu_ready, k - 1)
                for c in range(FC):
                    last = t.transpose(hT_ps[odd][:, c * P:(c + 1) * P], hs[odd][:, c * P:(c + 1) * P], ident[:])
                last.then_inc(hT_done, 1)

            def product2(k, odd):
                pe.wait_ge(gelu_ready, k + 1)
                need(pe, z_ready, k)
                for c in range(FC):
                    last = t.matmul(y_ps[:, 0:P], gs[odd][:, c * P:(c + 1) * P], w2s[:, bass.ds(w_off[k] + c * P, P)],
                                    start=(c == 0), stop=(c == FC - 1))
                last.then_inc(y_done, 1)

            def turn(i, odd):
                def on(k):
                    return not isinstance(i, int) or 0 <= k < NT
                if on(i + 2):
                    transpose_x(i + 2, odd)
                if on(i + 1):
                    product1(i + 1, 1 - odd)
                    attention(i + 1, 1 - odd)
                if on(i):
                    transpose_h(i, odd)
                if on(i - 1):
                    product2(i - 1, 1 - odd)

            pe.wait_ge(tables_ready, 1)
            w_off = offsets(mybir.EngineType.PE, w_at, (E - 1) * F)
            pe.wait_ge(w1_in, 16)
            pe.wait_ge(w2_in, 16)
            pe.wait_ge(mat_ready, 1)
            for i in range(-2, NT + 1):
                turn(i, i % 2)


_INS = ['L0_attn_x', 'L0_attn_norm_weight', 'L0_attn_w_qkv', 'L0_attn_temperature', 'L0_attn_w_out',
        'L0_ffn_Wr', 'L0_ffn_W1', 'L0_ffn_b1', 'L0_ffn_W2', 'L0_ffn_b2']
_OUTS = [((2, 1024, 128), 'float32')]


def kernel(**inputs):
    import numpy as _np
    import concourse.bacc as _bacc
    from concourse import mybir as _mybir
    from concourse.bass_utils import run_bass_kernel_spmd as _run

    nc = _bacc.Bacc("TRN2", target_bir_lowering=False, num_devices=1)
    arrays, args = {}, []
    for name in _INS:
        a = _np.ascontiguousarray(inputs[name])
        arrays[f"in_{name}_dram"] = a
        args.append(nc.dram_tensor(f"in_{name}_dram", a.shape, _mybir.dt.from_np(a.dtype), kind="ExternalInput").ap())
    for i, (shape, dtype) in enumerate(_OUTS):
        dt = _mybir.dt.from_np(_np.dtype(dtype))
        args.append(nc.dram_tensor(f"out_{i}_dram", shape, dt, kind="ExternalOutput").ap())
    build(nc, *args)
    r = _run(nc, [arrays], core_ids=[0])
    got = tuple(r.results[0][f"out_{i}_dram"] for i in range(len(_OUTS)))
    return got[0]
```

```python
from contextlib import ExitStack

import concourse.bass as bass
from concourse import mybir

F32 = mybir.dt.float32
BF16 = mybir.dt.bfloat16
I32 = mybir.dt.int32
ALU = mybir.AluOpType
ACT = mybir.ActivationFunctionType
AX_X = mybir.AxisListType.X
At = bass.IndirectOffsetOnAxis

P = 128
NB = 2
NJ = 16
JB = NJ // NB
T = P * NJ
E = 8
F = 512
FC = F // P
NT = T // P + E - 1
DH = 16
SHIFT = 7
WARM_UP = 5

RING = 4
NORM_DVE = (2, 3, 4)
FLIGHT = 4
XT_RING = 6
EARLY = 2
MAT_TURN = 3

SHIFTED, RSTD, RA, RB, HALF_P = P, P + 1, P + 2, P + 3, P + 4
ROW = P + 8

LN_EPS = 1e-5
RMS_EPS = 1e-6
NORM_FLOOR = 1e-12
OUTSIDE = 1e30
SLOT_CUTS = (0, 5)
SLOTS_POOL = 12
NOWHERE = 4 * T


def attention_of(turn):
    return [k for k in range(NT) if max(k + 1, MAT_TURN + k // 2) == turn]


def build(nc, x, norm_w, w_qkv, temperature, w_out, w_r, w1, b1, w2, b2, out):
    x_v = x.rearrange("b (p j) d -> b p j d", p=P)
    out_v = out.rearrange("b n d -> (b n) d")
    rows = nc.dram_tensor("token_rows", (T, ROW), F32).ap()
    rows_v = rows.rearrange("(b p j) r -> b p j r", b=NB, p=P)

    with ExitStack() as ctx:
        def sb(name, shape, dt=F32):
            return ctx.enter_context(nc.sbuf_tensor(name, shape, dt))

        def bank(name):
            return ctx.enter_context(nc.psum_tensor(name, [P, 512], F32))

        def sem(name):
            return ctx.enter_context(nc.semaphore(name))

        ident = sb("ident", [P, P])
        ones = sb("ones", [P, P])
        ones_bf = sb("ones_bf", [P, P], BF16)
        before = sb("before", [P, P], BF16)
        head_gap = sb("head_gap", [P, P])
        head_rows = sb("head_rows", [E, P])
        slot_iota = sb("slot_iota", [P, P], BF16)
        tile_iota = sb("tile_iota", [P, NT], BF16)
        tile_start = sb("tile_start", [P, NT])
        own_e = sb("own_e", [E, 1])
        rev_e = sb("rev_e", [P, E])
        earlier_e = sb("earlier_e", [P, E, E])
        id_p = sb("id_p", [P, NB])
        id_j = sb("id_j", [P, NJ], BF16)
        warm_row = sb("warm_row", [P, F], BF16)
        xe = sb("xe", [P, NJ, ROW])
        wqkv = sb("wqkv", [P, 3, P])
        wout = sb("wout", [P, P])
        nw = sb("nw", [P, 1])
        temp = sb("temp", [E, 1])
        wr = sb("wr", [P, E])
        w2s = sb("w2s", [P, E * F])
        b1s = sb("b1s", [E, F])
        b2s = sb("b2s", [P, E, P])
        stats = sb("stats", [P, NJ, 6])
        mv = sb("mv", [P, NJ, 2])
        v12 = sb("v12", [P, 2, NJ])
        root = sb("root", [P, 2, NJ])
        shift = sb("shift", [P, 2, NJ])
        rs = sb("rs", [P, 2, NJ])
        rt = sb("rt", [P, 2, NJ])
        xr = sb("xr", [P, NJ, P])
        xT = sb("xT", [P, NJ * P])
        wrc = sb("wrc", [P, E])
        lmax = sb("lmax", [P, NJ])
        is_max = sb("is_max", [P, NJ, E])
        best = sb("best", [P, NJ])
        chosen = sb("chosen", [P, NJ + 1, E], BF16)
        below = sb("below", [P, NJ, E])
        expo = sb("expo", [P, NJ, E])
        psum_e = sb("psum_e", [P, NJ])
        p_max = sb("p_max", [P, NJ])
        rfac = sb("rfac", [P, NJ])
        tiles_i = sb("tiles_i", [P, 2, E], I32)
        ee = sb("ee", [P, E, E])
        base = sb("base", [P, E])
        place = sb("place", [P, NJ, E])
        pos_i = sb("pos_i", [P, NJ], I32)
        ab_i = sb("ab_i", [P, 2, NJ], I32)
        ab = sb("ab", [P, 2, NJ], BF16)
        in_tile = sb("in_tile", [P, NJ, NT], BF16)
        tagged = sb("tagged", [P, NJ, 2, NT], BF16)
        in_slot = sb("in_slot", [P, NJ, P], BF16)
        late = sb("late", [P, NT])
        token1 = sb("token1", [P, NT])
        from_row = sb("from_row", [P, NT], I32)
        to_row = sb("to_row", [P, NT], I32)
        et = sb("et", [P, NT, E - 1])
        ef = sb("ef", [P, NT])
        of_e = sb("of_e", [E, NT])
        e128_at = sb("e128_at", [1, NT], I32)
        e512_at = sb("e512_at", [1, NT], I32)
        b1t = sb("b1t", [P, FC, NT])
        wqkT = sb("wqkT", [P, 2 * P])
        woutT = sb("woutT", [P, P])
        gram = sb("gram", [P, NB, P])
        gw = sb("gw", [P, NB, 2 * P])
        prod = sb("prod", [P, NB, 2 * P])
        n2 = sb("n2", [P, NB * P + NB])
        ni = sb("ni", [P, NB * P + NB])
        nt_ = sb("nt_", [P, NB * P + NB])
        etemp = sb("etemp", [P, 1])
        qscale = sb("qscale", [P, NB])
        sim = sb("sim", [P, NB, P])
        smin = sb("smin", [P, NB])
        prob = sb("prob", [P, NB, P])
        psumA = sb("psumA", [P, NB])
        pinv = sb("pinv", [P, NB])
        att = sb("att", [P, NB, P])
        mid = sb("mid", [P, NB, P])
        mat = sb("mat", [P, NB * P])
        xg = sb("xg", [P, NT, ROW])
        sg = sb("sg", [P, NT, P])
        xns = [sb(f"xns{i}", [P, P]) for i in range(2)]
        xTs = [sb(f"xTs{i}", [P, P]) for i in range(XT_RING)]
        w1r = [sb(f"w1r{i}", [P, F]) for i in range(RING)]
        gs = [sb(f"gs{i}", [P, F]) for i in range(2)]
        zs = [sb(f"zs{i}", [P, P]) for i in range(2)]
        th = [sb(f"th{i}", [P, P]) for i in range(2)]
        qs = [sb(f"qs{i}", [P, P]) for i in range(RING)]
        us = sb("us", [P, P])

        banks = [bank(f"bank{i}") for i in range(8)]
        hT_ps, xT_ps, y_ps, s_ps = banks[4:6], banks[6:8], (banks[0], banks[3]), banks[1:3]
        logits_ps = banks[4][:, 0:NJ * E].rearrange("p (j e) -> p j e", e=E)
        rank_ps = banks[5][:, 0:(NJ + 1) * E].rearrange("p (j e) -> p j e", e=E)
        wmean_ps, temp_ps = banks[6][:, 0:E], banks[6][:, E:E + 1]
        slots_ps = banks[6][:, 0:2 * NT].rearrange("p (g t) -> p g t", g=2)
        wT_ps = banks[7]
        gram_ps = banks[7][:, 0:NB * P].rearrange("p (b c) -> p b c", b=NB)
        gw_ps = banks[0][:, :].rearrange("p (b c) -> p b c", b=NB)
        sim_ps = banks[1][:, 0:NB * P].rearrange("p (b c) -> p b c", b=NB)
        norm_ps = banks[2][:, 0:NB * P + NB]
        b1_ps = banks[3][:, 0:FC * NT].rearrange("p (c t) -> p c t", c=FC)
        mid_ps = banks[3][:, 0:NB * P].rearrange("p (b c) -> p b c", b=NB)
        mat_ps = banks[2][:, 0:NB * P].rearrange("p (b c) -> p b c", b=NB)

        x_in = [sem(f"x_in{i}") for i in range(NJ // 4)]
        att_w_in = sem("att_w_in")
        wr_in = sem("wr_in")
        w1_in = [sem(f"w1_in{i}") for i in range(RING)]
        w2_in, b1_in, b2_in = sem("w2_in"), sem("b1_in"), sem("b2_in")
        rows_out = sem("rows_out")
        row_in = [sem(f"row_in{i}") for i in range(FLIGHT)]
        result_out = sem("result_out")
        pool_step, dve_step = sem("pool_step"), sem("dve_step")
        warm_ready, ident_ready, const_ready = sem("warm_ready"), sem("ident_ready"), sem("const_ready")
        var_ready, root_ready, rs_ready = sem("var_ready"), sem("root_ready"), sem("rs_ready")
        shift_ready = sem("shift_ready")
        wmean_done, wrc_ready, ln_ready = sem("wmean_done"), sem("wrc_ready"), sem("ln_ready")
        xT_tok_done, xT_tok_ready = sem("xT_tok_done"), sem("xT_tok_ready")
        xr_pool, xr_act = sem("xr_pool"), sem("xr_act")
        logits_done, below_ready, expo_ready = sem("logits_done"), sem("below_ready"), sem("expo_ready")
        chosen_ready, rank_done, tags_ready = sem("chosen_ready"), sem("rank_done"), sem("tags_ready")
        in_slot_ready, in_slot_pool, slots_done = sem("in_slot_ready"), sem("in_slot_pool"), sem("slots_done")
        ab_ready, in_tile_ready, id_tags_ready = sem("ab_ready"), sem("in_tile_ready"), sem("id_tags_ready")
        scalars_ready, from_ready, to_ready, tables_ready = (
            sem("scalars_ready"), sem("from_ready"), sem("to_ready"), sem("tables_ready"))
        b1t_done, b1t_ready = sem("b1t_done"), sem("b1t_ready")
        wT_done, wT_ready, temp_done = sem("wT_done"), sem("wT_ready"), sem("temp_done")
        gram_done, gram_ready, gw_done, gw_ready = sem("gram_done"), sem("gram_ready"), sem("gw_done"), sem("gw_ready")
        prod_ready, norm_done, n2_ready = sem("prod_ready"), sem("norm_done"), sem("n2_ready")
        nln_ready, nroot_ready, etemp_ready = sem("nln_ready"), sem("nroot_ready"), sem("etemp_ready")
        sim_ready, prob_ready, att_ready = sem("sim_ready"), sem("prob_ready"), sem("att_ready")
        mid_done, mid_ready, mat_done, mat_ready = sem("mid_done"), sem("mid_ready"), sem("mat_done"), sem("mat_ready")
        xn_ready, xT_done, xT_ready = sem("xn_ready"), sem("xT_done"), sem("xT_ready")
        xT_early = sem("xT_early")
        xn_dve = sem("xn_dve")
        hT_done, gelu_ready = sem("hT_done"), sem("gelu_ready")
        s_done, s0_ready, s_ready = sem("s_done"), sem("s0_ready"), sem("s_ready")
        y_done, z_ready, tanh_ready = sem("y_done"), sem("z_ready"), sem("tanh_ready")
        q_done, u_done, o_ready = sem("q_done"), sem("u_done"), sem("o_ready")

        def need(eng, semaphore, value):
            if not isinstance(value, int) or value > 0:
                eng.wait_ge(semaphore, value)

        biases = b2s[:].rearrange("p e d -> p (e d)")
        w1_v = w1.rearrange("e d f -> (e d) f")

        def offsets(engine, table, most):
            return nc.values_load_multi_w_load_instructions(
                table[0:1, :], engines=[engine], min_val=0, max_val=most, 
                skip_runtime_bounds_check_because="an expert is 0 to 7 by its construction")[1]

        block = ctx.enter_context(nc.Block())

        @block.sync
        def _(sp):
            for i in range(NJ // 4):
                j = i * 4 % JB
                sp.dma_start(xe[:, i * 4:(i + 1) * 4, 0:P], x_v[i * 4 // JB, :, j:j + 4, :]).then_inc(x_in[i], 16)
            sp.dma_start(wqkv[:], w_qkv.rearrange("(s o) c -> o s c", s=3)).then_inc(att_w_in, 16)
            sp.dma_start(wout[:], w_out).then_inc(att_w_in, 16)
            sp.dma_start(w2s[:].rearrange("f (e c d) -> f e c d", e=E, c=FC),
                         w2.rearrange("e (c f) d -> f e c d", c=FC)).then_inc(w2_in, 16)
            sp.dma_start(b1s[:], b1).then_inc(b1_in, 16)
            sp.dma_start(b2s[:], b2.partition_broadcast(P)).then_inc(b2_in, 16)
            sp.wait_ge(scalars_ready, 1)
            for b in range(NB):
                sp.dma_start(rows_v[b], xe[:, b * JB:(b + 1) * JB, :]).then_inc(rows_out, 16)
            sp.wait_ge(tables_ready, 1)
            row_off = offsets(mybir.EngineType.SP, e128_at, (E - 1) * P)
            for k in range(NT):
                need(sp, hT_done, k - RING + 1)
                sp.dma_start(w1r[k % RING][:], w1_v[bass.ds(row_off[k], P), :]).then_inc(w1_in[k % RING], 16)

        @block.gpsimd
        def _(pool):
            steps = [0]

            def link(ins):
                steps[0] += 1
                ins.then_inc(pool_step, 1)
                pool.wait_ge(pool_step, steps[0])

            g = nc.gpsimd
            g.memset(ones_bf[:], 1.0)
            g.memset(warm_row[:], 0.0).then_inc(warm_ready, 1)
            link(g.memset(ones[:], 1.0))
            (g.affine_select(out=ident[:], in_=ones[:], compare_op=ALU.is_equal, fill=0.0, base=0,
                                 pattern=[[-1, P]], channel_multiplier=1)).then_inc(ident_ready, 1)
            g.memset(xe[:, :, SHIFTED:ROW], 0.0)
            g.memset(chosen[:, NJ:NJ + 1, :], 0.0)
            g.affine_select(out=before[:], in_=ones[:], compare_op=ALU.is_gt, fill=0.0, base=0,
                            pattern=[[1, P]], channel_multiplier=-1)
            g.iota(slot_iota[:], [[1, P]], base=0, channel_multiplier=0, allow_small_or_imprecise_dtypes=True)
            g.iota(tile_iota[:], [[1, NT]], base=0, channel_multiplier=0, allow_small_or_imprecise_dtypes=True)
            g.iota(tile_start[:], [[P, NT]], base=0, channel_multiplier=0, allow_small_or_imprecise_dtypes=True)
            g.iota(own_e[:], [[0, 1]], base=0, channel_multiplier=1, allow_small_or_imprecise_dtypes=True)
            g.iota(rev_e[:], [[-1, E]], base=E, channel_multiplier=0, allow_small_or_imprecise_dtypes=True)
            g.iota(id_p[:], [[T // NB, NB]], base=0, channel_multiplier=JB, allow_small_or_imprecise_dtypes=True)
            g.iota(id_j[:], [[0, NB], [1, JB]], base=1, channel_multiplier=0, allow_small_or_imprecise_dtypes=True)
            link(g.memset(earlier_e[:], float(P)))
            g.affine_select(out=earlier_e[:], in_=earlier_e[:], compare_op=ALU.is_gt, fill=0.0, base=0,
                            pattern=[[1, E], [-1, E]], channel_multiplier=0)
            link(g.memset(head_gap[:], 0.0))
            gap = head_gap[:].rearrange("p (h i) -> p h i", i=DH)
            link(g.affine_select(out=gap, in_=gap, compare_op=ALU.is_ge, fill=OUTSIDE, base=0,
                                 pattern=[[-DH, E], [0, DH]], channel_multiplier=1))
            link(g.affine_select(out=gap, in_=gap, compare_op=ALU.is_ge, fill=OUTSIDE, base=DH - 1,
                                 pattern=[[DH, E], [0, DH]], channel_multiplier=-1))
            hr = head_rows[:].rearrange("p (h i) -> p h i", i=DH)
            g.affine_select(out=hr, in_=ones[0:E, :].rearrange("p (h i) -> p h i", i=DH), compare_op=ALU.is_equal,
                            fill=0.0, base=0, pattern=[[-1, E], [0, DH]], channel_multiplier=1
                            ).then_inc(const_ready, 1)

            pool.wait_ge(rs_ready, 1)
            pool.wait_ge(shift_ready, 1)
            for j in range(0, NJ, 2):
                g.tensor_scalar(xr[:, j, :], xe[:, j, 0:P], rs[:, 1, j:j + 1], shift[:, 1, j:j + 1],
                                ALU.mult, ALU.add).then_inc(xr_pool, 1)

            pool.wait_ge(ab_ready, 1)
            for j in range(SLOTS_POOL, NJ):
                g.tensor_scalar(in_slot[:, j, :], slot_iota[:], ab_i[:, 1, j:j + 1], None, ALU.is_equal
                                ).then_inc(in_slot_pool, 1)
            pool.wait_ge(rows_out, 16 * NB)
            pool.wait_ge(from_ready, 1)
            for k in range(NT):
                if k >= FLIGHT:
                    pool.wait_ge(row_in[k % FLIGHT], 16 * (k // FLIGHT))
                g.indirect_dma_start(xg[:, k, :], None, rows, At(ap=from_row[:, k:k + 1], axis=0)
                                     ).then_inc(row_in[k % FLIGHT], 16)
            pool.wait_ge(to_ready, 1)
            for k in range(NT):
                pool.wait_ge(o_ready, k + 1)
                g.indirect_dma_start(out_v, At(ap=to_row[:, k:k + 1], axis=0), xg[:, k, 0:P], None,
                                     bounds_check=T - 1, oob_is_err=False).then_inc(result_out, 16)
            pool.wait_ge(result_out, 16 * NT)

        @block.vector
        def _(dve):
            v = nc.vector
            steps = [0]

            def link(ins):
                steps[0] += 1
                ins.then_inc(dve_step, 1)
                dve.wait_ge(dve_step, steps[0])

            def mark(ins):
                steps[0] += 1
                ins.then_inc(dve_step, 1)
                return steps[0]

            def after(count):
                dve.wait_ge(dve_step, count)

            for j in range(NJ):
                if j % 4 == 0:
                    dve.wait_ge(x_in[j // 4], 16)
                if j == 2:
                    dve.wait_ge(wmean_done, 1)
                    v.scalar_tensor_tensor(out=wrc[:], in0=wmean_ps, scalar=-1.0 / P, in1=wr[:],
                                           op0=ALU.mult, op1=ALU.add).then_inc(wrc_ready, 1)
                last = v.bn_stats(stats[:, j, :], xe[:, j, 0:P])
            link(last)
            for j in range(NJ):
                last = v.bn_aggr(mv[:, j, :], stats[:, j, :])
            link(last)
            var = mv[:, :, 1]
            v.tensor_scalar(v12[:, 0, :], var, LN_EPS, None, ALU.add)
            v.tensor_scalar(v12[:, 1, :], var, 1.0 + RMS_EPS, RMS_EPS * LN_EPS, ALU.mult, ALU.add
                            ).then_inc(var_ready, 1)
            dve.wait_ge(const_ready, 1)
            dve.wait_ge(logits_done, 1)
            rev = rev_e[:].unsqueeze(1).to_broadcast([P, NJ, E])
            max_at = mark(v.tensor_reduce(lmax[:], logits_ps, AX_X, ALU.max))
            dve.wait_ge(var_ready, 1)
            dve.wait_ge(root_ready, 1)
            root_at = mark(v.scalar_tensor_tensor(out=rt[:], in0=root[:], scalar=-0.5, in1=root[:], op0=ALU.mult, op1=ALU.mult))
            after(max_at)
            max_at = mark(v.tensor_tensor(is_max[:], logits_ps, lmax[:].unsqueeze(2).to_broadcast([P, NJ, E]),
                                          ALU.is_equal))
            after(root_at)
            root_at = mark(v.tensor_tensor(rt[:], rt[:], v12[:], ALU.mult))
            after(max_at)
            max_at = mark(v.tensor_tensor(is_max[:], is_max[:], rev, ALU.mult))
            after(root_at)
            v.scalar_tensor_tensor(out=rs[:], in0=rt[:], scalar=1.5, in1=root[:], op0=ALU.add, op1=ALU.mult
                                   ).then_inc(rs_ready, 1)
            after(max_at)
            max_at = mark(v.tensor_reduce(best[:], is_max[:], AX_X, ALU.max))
            dve.wait_ge(rs_ready, 1)
            v.scalar_tensor_tensor(out=shift[:], in0=mv[:, :, 0].unsqueeze(1).to_broadcast([P, 2, NJ]), scalar=-1.0,
                                   in1=rs[:], op0=ALU.mult, op1=ALU.mult).then_inc(shift_ready, 1)
            after(max_at)
            v.tensor_tensor(chosen[:, 0:NJ, :], rev, best[:].unsqueeze(2).to_broadcast([P, NJ, E]), ALU.is_equal
                            ).then_inc(chosen_ready, 1)
            below_at = mark(v.tensor_tensor(below[:], logits_ps, lmax[:].unsqueeze(2).to_broadcast([P, NJ, E]),
                                            ALU.subtract))
            rfac_at = mark(v.tensor_tensor(rfac[:], rs[:, 0, :], v12[:, 0, :], ALU.mult))
            after(below_at)
            v.tensor_tensor(below[:], below[:], rs[:, 0, :].unsqueeze(2).to_broadcast([P, NJ, E]), ALU.mult
                            ).then_inc(below_ready, 1)
            after(rfac_at)
            link(v.tensor_tensor(rfac[:], rfac[:], rs[:, 1, :], ALU.mult))
            dve.wait_ge(shift_ready, 1)
            v.tensor_copy(xe[:, :, SHIFTED], shift[:, 0, :])
            v.tensor_copy(xe[:, :, RSTD], rs[:, 0, :])

            dve.wait_ge(rank_done, 1)
            dve.wait_ge(chosen_ready, 1)
            place_at = mark(v.tensor_scalar(tiles_i[:, 0, :], rank_ps[:, NJ, :], float(P - 1), None, ALU.add))
            dve.wait_ge(expo_ready, 1)
            p_at = mark(v.tensor_reduce(psum_e[:], expo[:], AX_X, ALU.add))
            after(place_at)
            place_at = mark(v.tensor_scalar(tiles_i[:, 1, :], tiles_i[:, 0, :], SHIFT, None, ALU.arith_shift_right))
            after(p_at)
            p_at = mark(v.reciprocal(p_max[:], psum_e[:]))
            after(place_at)
            place_at = mark(v.tensor_tensor(ee[:], earlier_e[:], tiles_i[:, 1, :].unsqueeze(1).to_broadcast([P, E, E]),
                                            ALU.mult))
            after(p_at)
            v.tensor_scalar(xe[:, :, HALF_P], p_max[:], 0.5, None, ALU.mult)
            after(place_at)
            place_at = mark(v.tensor_reduce(base[:], ee[:], AX_X, ALU.add))
            for b, at in enumerate((RA, RB)):
                half = slice(b * JB, (b + 1) * JB)
                last = v.scalar_tensor_tensor(out=xe[:, half, at], in0=p_max[:, half], scalar=0.5, in1=rfac[:, half],
                                              op0=ALU.mult, op1=ALU.mult)
            last.then_inc(scalars_ready, 1)
            after(place_at)
            et_at = mark(v.tensor_tensor(et[:], base[:, 1:E].unsqueeze(1).to_broadcast([P, NT, E - 1]),
                                         tile_start[:].unsqueeze(2).to_broadcast([P, NT, E - 1]), ALU.is_le))
            place_at = mark(v.tensor_tensor(place[:], rank_ps[:, 0:NJ, :], base[:].unsqueeze(1).to_broadcast([P, NJ, E]), ALU.add))
            after(et_at)
            et_at = mark(v.tensor_reduce(ef[:], et[:], AX_X, ALU.add))
            after(place_at)
            place_at = mark(v.tensor_tensor(place[:], place[:], chosen[:, 0:NJ, :], ALU.mult))
            after(et_at)
            v.tensor_scalar(e128_at[:], ef[0:1, :], float(P), None, ALU.mult)
            after(place_at)
            with nc.allow_low_precision(reason="sums of whole numbers below 2**24, and int32 holds them"):
                place_at = mark(v.tensor_reduce(pos_i[:], place[:], AX_X, ALU.add))
            v.tensor_scalar(e512_at[:], ef[0:1, :], float(F), None, ALU.mult)
            v.tensor_scalar(of_e[:], ef[0:E, :], own_e[:, 0:1], None, ALU.is_equal).then_inc(tables_ready, 1)
            after(place_at)
            v.tensor_scalar(ab_i[:, 0, :], pos_i[:], SHIFT, None, ALU.arith_shift_right)
            link(v.tensor_scalar(ab_i[:, 1, :], pos_i[:], P - 1, None, ALU.bitwise_and))
            v.tensor_copy(ab[:], ab_i[:]).then_inc(ab_ready, 1)
            dve.wait_ge(ab_ready, 1)
            v.tensor_tensor(in_tile[:], ab[:, 0, :].unsqueeze(2).to_broadcast([P, NJ, NT]),
                            tile_iota[:].unsqueeze(1).to_broadcast([P, NJ, NT]), ALU.is_equal).then_inc(in_tile_ready, 1)
            for lo, hi in zip(SLOT_CUTS, SLOT_CUTS[1:] + (SLOTS_POOL,)):
                v.tensor_tensor(in_slot[:, lo:hi, :], ab[:, 1, lo:hi].unsqueeze(2).to_broadcast([P, hi - lo, P]),
                                slot_iota[:].unsqueeze(1).to_broadcast([P, hi - lo, P]), ALU.is_equal
                                ).then_inc(in_slot_ready, 1)
                if lo == 0:
                    dve.wait_ge(in_tile_ready, 1)
                    v.tensor_tensor(tagged[:, :, 1, :], in_tile[:], id_j[:].unsqueeze(2).to_broadcast([P, NJ, NT]),
                                    ALU.mult).then_inc(tags_ready, 1)
            for b in range(NB):
                dve.wait_ge(gw_ready, 1)
                v.tensor_tensor(prod[:, b, :], gw[:, b, :], wqkT[:], ALU.mult).then_inc(prod_ready, 1)
            dve.wait_ge(slots_done, 1)
            link(v.tensor_copy(late[:], slots_ps[:, 1, :]))
            link(v.tensor_tensor(token1[:], late[:], slots_ps[:, 0, :], ALU.add))
            v.tensor_scalar(from_row[:], token1[:], -1.0, 0.0, ALU.add, ALU.max).then_inc(from_ready, 1)
            dve.wait_ge(norm_done, 1)
            v.tensor_scalar(n2[:], norm_ps, NORM_FLOOR * NORM_FLOOR, None, ALU.max).then_inc(n2_ready, 1)
            link(v.tensor_scalar(late[:], token1[:], 0.0, float(NOWHERE), ALU.is_equal, ALU.mult))
            link(v.tensor_tensor(token1[:], late[:], token1[:], ALU.add))
            v.tensor_scalar(to_row[:], token1[:], -1.0, None, ALU.add).then_inc(to_ready, 1)

            dve.wait_ge(n2_ready, 1)
            dve.wait_ge(nroot_ready, 1)
            link(v.scalar_tensor_tensor(out=nt_[:], in0=ni[:], scalar=-0.5, in1=ni[:], op0=ALU.mult, op1=ALU.mult))
            link(v.tensor_tensor(nt_[:], nt_[:], n2[:], ALU.mult))
            link(v.scalar_tensor_tensor(out=ni[:], in0=nt_[:], scalar=1.5, in1=ni[:], op0=ALU.add, op1=ALU.mult))
            dve.wait_ge(etemp_ready, 1)
            link(v.tensor_scalar(qscale[:], ni[:, NB * P:], etemp[:, 0:1], -1.0, ALU.mult, ALU.mult))
            for b in range(NB):
                last = v.scalar_tensor_tensor(out=sim[:, b, :], in0=sim_ps[:, b, :], scalar=qscale[:, b:b + 1],
                                              in1=ni[:, b * P:(b + 1) * P], op0=ALU.mult, op1=ALU.mult)
            link(last)
            link(v.tensor_tensor(sim[:], sim[:], head_gap[:].unsqueeze(1).to_broadcast([P, NB, P]), ALU.add))
            v.tensor_reduce(smin[:], sim[:], AX_X, ALU.min).then_inc(sim_ready, 1)
            dve.wait_ge(prob_ready, 1)
            link(v.reciprocal(pinv[:], psumA[:]))
            for b in range(NB):
                last = v.tensor_scalar(att[:, b, :], prob[:, b, :], pinv[:, b:b + 1], None, ALU.mult)
            last.then_inc(att_ready, 1)
            def keep_xT(k):
                dve.wait_ge(xT_done, k + 1)
                need(dve, s_done, k - XT_RING + 1)
                v.tensor_copy(xTs[k % XT_RING][:], xT_ps[k % 2][:, 0:P]).then_inc(xT_ready, 1)

            def normalise(k):
                dve.wait_ge(row_in[k % FLIGHT], 16 * (k // FLIGHT + 1))
                dve.wait_ge(xT_done, k - 1)
                v.tensor_scalar(xns[k % 2][:], xg[:, k, 0:P], xg[:, k, RSTD:RSTD + 1], xg[:, k, SHIFTED:SHIFTED + 1],
                                ALU.mult, ALU.add).then_inc(xn_dve, 1)

            def attention(k):
                dve.wait_ge(s0_ready, k + 1)
                row = xg[:, bass.ds(k, 1), :].rearrange("p a r -> p (a r)")
                acc = sg[:, bass.ds(k, 1), :].rearrange("p a r -> p (a r)")
                v.scalar_tensor_tensor(out=acc, in0=s_ps[k % 2][:, P:2 * P], scalar=row[:, RB:RB + 1], in1=acc,
                                       op0=ALU.mult, op1=ALU.add).then_inc(s_ready, 1)

            def ffn_out(k, odd):
                dve.wait_ge(y_done, k + 1)
                v.tensor_tensor(zs[odd][:], y_ps[odd][:, 0:P], biases[:, bass.ds(b_off[k], P)], ALU.add).then_inc(z_ready, 1)

            def gate(k, odd):
                dve.wait_ge(tanh_ready, k + 1)
                need(dve, u_done, k - RING + 1)
                v.scalar_tensor_tensor(out=qs[k % RING][:], in0=th[odd][:], scalar=1.0, in1=zs[odd][:],
                                       op0=ALU.add, op1=ALU.mult).then_inc(q_done, 1)

            def times_attention(k):
                acc = sg[:, bass.ds(k, 1), :].rearrange("p a r -> p (a r)")
                dve.wait_ge(q_done, k + 1)
                dve.wait_ge(s_ready, k + 1)
                need(dve, o_ready, k)
                v.tensor_tensor(us[:], qs[k % RING][:], acc, ALU.mult).then_inc(u_done, 1)

            def add_x(k):
                row = xg[:, bass.ds(k, 1), :].rearrange("p a r -> p (a r)")
                dve.wait_ge(u_done, k + 1)
                v.tensor_tensor(row[:, 0:P], us[:], row[:, 0:P], ALU.add).then_inc(o_ready, 1)

            def turn(i, odd):
                def on(k):
                    return 0 <= k < NT
                if i + 3 in NORM_DVE:
                    normalise(i + 3)
                if EARLY <= i + 2 < NT:
                    keep_xT(i + 2)
                for k in attention_of(i - 1):
                    attention(k)
                if on(i - 2):
                    gate(i - 2, odd)
                for k in attention_of(i - 1):
                    times_attention(k)
                    add_x(k)
                if on(i - 1):
                    ffn_out(i - 1, 1 - odd)

            dve.wait_ge(b2_in, 16)
            dve.wait_ge(tables_ready, 1)
            b_off = offsets(mybir.EngineType.DVE, e128_at, (E - 1) * P)
            normalise(2)
            for i in range(0, NT + 2):
                turn(i, i % 2)

        @block.scalar
        def _(act):
            a = nc.scalar
            act.dma_start(wr[:], w_r).then_inc(wr_in, 16)
            act.dma_start(nw[:], norm_w.rearrange("(c a) -> c a", a=1)).then_inc(att_w_in, 16)
            act.dma_start(temp[:], temperature.rearrange("h a b -> h (a b)")).then_inc(att_w_in, 16)
            a.preload_act_table_set("natural_log_exp_and_others")
            for g4 in range(4):
                act.wait_ge(xT_tok_done, g4 + 1)
                a.activation(xT[:, g4 * F:(g4 + 1) * F], banks[g4][:], ACT.Copy).then_inc(xT_tok_ready, 1)
            act.wait_ge(var_ready, 1)
            a.activation(root[:], v12[:], ACT.Ln).then_inc(ln_ready, 1)
            act.wait_ge(ln_ready, 1)
            a.activation(root[:], root[:], ACT.Exp, scale=-0.5).then_inc(root_ready, 1)
            act.wait_ge(wT_done, 1)
            act.wait_ge(att_w_in, 64)
            a.activation(wqkT[:], wT_ps[:, 0:2 * P], ACT.Copy, scale=nw[:, 0:1])
            a.activation(woutT[:], wT_ps[:, 2 * P:3 * P], ACT.Copy).then_inc(wT_ready, 1)
            act.wait_ge(temp_done, 1)
            a.activation(etemp[:], temp_ps, ACT.Exp).then_inc(etemp_ready, 1)
            act.wait_ge(rs_ready, 1)
            act.wait_ge(shift_ready, 1)
            for j in range(1, NJ, 2):
                a.activation(xr[:, j, :], xe[:, j, 0:P], ACT.Identity, bias=shift[:, 1, j:j + 1],
                             scale=rs[:, 1, j:j + 1]).then_inc(xr_act, 1)
                if j == 3:
                    act.wait_ge(below_ready, 1)
                    a.activation(expo[:], below[:], ACT.Exp).then_inc(expo_ready, 1)
            act.wait_ge(gram_done, NB)
            a.activation(gram[:], gram_ps, ACT.Copy).then_inc(gram_ready, 1)
            act.wait_ge(in_tile_ready, 1)
            for b in range(NB):
                half = slice(b * JB, (b + 1) * JB)
                last = a.activation(tagged[:, half, 0, :], in_tile[:, half, :], ACT.Copy, scale=id_p[:, b:b + 1])
            last.then_inc(id_tags_ready, 1)
            act.wait_ge(gw_done, 1)
            a.activation(gw[:], gw_ps, ACT.Copy).then_inc(gw_ready, 1)
            act.wait_ge(n2_ready, 1)
            a.activation(ni[:], n2[:], ACT.Ln).then_inc(nln_ready, 1)
            act.wait_ge(nln_ready, 1)
            a.activation(ni[:], ni[:], ACT.Exp, scale=-0.5).then_inc(nroot_ready, 1)
            act.wait_ge(b1t_done, 1)
            a.activation(b1t[:], b1_ps, ACT.Copy).then_inc(b1t_ready, 1)

            def normalise(k, odd):
                act.wait_ge(row_in[k % FLIGHT], 16 * (k // FLIGHT + 1))
                need(act, xT_done, k - 1)
                a.activation(xns[odd][:], xg[:, k, 0:P], ACT.Identity, bias=xg[:, k, SHIFTED:SHIFTED + 1],
                             scale=xg[:, k, RSTD:RSTD + 1]).then_inc(xn_ready, 1)

            def attention(k):
                act.wait_ge(s_done, k + 1)
                a.activation(sg[:, bass.ds(k, 1), :].rearrange("p a r -> p (a r)"), s_ps[k % 2][:, 0:P], ACT.Copy,
                             scale=xg[:, bass.ds(k, 1), RA:RA + 1].rearrange("p a r -> p (a r)")
                             ).then_inc(s0_ready, 1)

            def gelu(k, odd, chunks):
                act.wait_ge(hT_done, k + 1)
                need(act, y_done, k - 1)
                for c in chunks:
                    last = a.activation(gs[odd][:, c * P:(c + 1) * P], hT_ps[odd][:, c * P:(c + 1) * P], ACT.Gelu,
                                        bias=b1t[:, c, k:k + 1])
                if c == FC - 1:
                    last.then_inc(gelu_ready, 1)

            def tanh(k, odd):
                act.wait_ge(z_ready, k + 1)
                need(act, q_done, k - 1)
                a.activation(th[odd][:], zs[odd][:], ACT.Tanh,
                             scale=xg[:, bass.ds(k, 1), HALF_P:HALF_P + 1].rearrange("p a r -> p (a r)")
                             ).then_inc(tanh_ready, 1)

            def turn(i, odd):
                def on(k):
                    return not isinstance(i, int) or 0 <= k < NT
                for k in attention_of(i - 1):
                    attention(k)
                if on(i + 3) and i + 3 not in NORM_DVE:
                    normalise(i + 3, 1 - odd)
                if on(i):
                    gelu(i, odd, range(FC // 2))
                if on(i - 2):
                    tanh(i - 2, odd)
                if on(i):
                    gelu(i, odd, range(FC // 2, FC))

            def keep_early(k):
                act.wait_ge(xT_done, k + 1)
                a.activation(xTs[k][:], xT_ps[k % 2][:, 0:P], ACT.Copy).then_inc(xT_early, 1)

            normalise(0, 0)
            normalise(1, 1)
            keep_early(0)
            keep_early(1)
            act.wait_ge(sim_ready, 1)
            for b in range(NB):
                last = a.activation(prob[:, b, :], sim[:, b, :], ACT.Exp, bias=smin[:, b:b + 1], scale=-1.0,
                                    accum_out=psumA[:, b:b + 1])
            last.then_inc(prob_ready, 1)
            a.preload_act_table_set("gelu_and_others")
            act.wait_ge(mid_done, 1)
            a.activation(mid[:], mid_ps, ACT.Copy).then_inc(mid_ready, 1)
            act.wait_ge(b1t_ready, 1)
            turn(0, 0)
            act.wait_ge(mat_done, 1)
            a.activation(mat[:].rearrange("p (b c) -> p b c", b=NB), mat_ps, ACT.Copy, scale=nw[:, 0:1]
                         ).then_inc(mat_ready, 1)
            for i in range(1, NT + 2):
                turn(i, i % 2)

        @block.tensor
        def _(pe):
            t = nc.tensor
            pe.wait_ge(warm_ready, 1)
            def keep_warm(count, bank):
                for _ in range(count):
                    t.matmul(bank[:], ones_bf[:], warm_row[:], start=True, stop=True)

            keep_warm(5, banks[7])
            pe.wait_ge(ident_ready, 1)

            def transposes(g4):
                pe.wait_ge(x_in[g4], 16)
                for j in range(g4 * 4, g4 * 4 + 4):
                    last = t.transpose(banks[g4][:, (j % 4) * P:(j % 4 + 1) * P], xe[:, j, 0:P], ident[:])
                last.then_inc(xT_tok_done, 1)

            def logits(g4):
                pe.wait_ge(xT_tok_ready, g4 + 1)
                for j in range(g4 * 4, g4 * 4 + 4):
                    last = t.matmul(logits_ps[:, j, :], xT[:, j * P:(j + 1) * P], wrc[:], start=True, stop=True)
                if g4 == 3:
                    last.then_inc(logits_done, 1)

            transposes(0)
            pe.wait_ge(wr_in, 16)
            t.matmul(wmean_ps, ones[:], wr[:], start=True, stop=True).then_inc(wmean_done, 1)
            transposes(1)
            transposes(2)
            transposes(3)
            pe.wait_ge(wrc_ready, 1)
            for g4 in range(4):
                logits(g4)
            pe.wait_ge(att_w_in, 64)
            t.transpose(wT_ps[:, 0:P], wqkv[:, 0, :], ident[:])
            t.transpose(wT_ps[:, P:2 * P], wqkv[:, 1, :], ident[:])
            t.transpose(wT_ps[:, 2 * P:3 * P], wout[:], ident[:]).then_inc(wT_done, 1)
            pe.wait_ge(const_ready, 1)
            t.matmul(temp_ps, head_rows[:], temp[:], start=True, stop=True).then_inc(temp_done, 1)

            def grams(b):
                for j in range(b * JB, (b + 1) * JB):
                    pe.wait_ge(xr_act if j % 2 else xr_pool, j // 2 + 1)
                    last = t.matmul(gram_ps[:, b, :], xr[:, j, :], xr[:, j, :],
                                    start=(j == b * JB), stop=(j == (b + 1) * JB - 1))
                last.then_inc(gram_done, 1)

            keep_warm(3, banks[0])
            pe.wait_ge(chosen_ready, 1)
            t.matmul(rank_ps, before[:], chosen[:], start=True, stop=False, skip_group_check=True)
            for c in range(1, NJ + 1):
                last = t.matmul(rank_ps[:, c:, :], ones_bf[:], chosen[:, 0:NJ + 1 - c, :], start=False,
                                stop=(c == NJ), skip_group_check=True)
            last.then_inc(rank_done, 1)
            pe.wait_ge(wT_ready, 1)
            grams(0)
            grams(1)
            pe.wait_ge(gram_ready, 1)
            for b in range(NB):
                done = t.matmul(gw_ps[:, b, :], gram[:, b, :], wqkT[:], start=True, stop=True)
            done.then_inc(gw_done, 1)
            pe.wait_ge(etemp_ready, 1)
            pe.wait_ge(tags_ready, 1)
            pe.wait_ge(id_tags_ready, 1)
            for j in range(NJ):
                if j in SLOT_CUTS:
                    pe.wait_ge(in_slot_ready, SLOT_CUTS.index(j) + 1)
                if j >= SLOTS_POOL:
                    pe.wait_ge(in_slot_pool, j - SLOTS_POOL + 1)
                last = t.matmul(slots_ps, in_slot[:, j, :], tagged[:, j, :, :], start=(j == 0), stop=(j == NJ - 1))
            last.then_inc(slots_done, 1)
            pe.wait_ge(gw_ready, 1)
            for b in range(NB):
                t.matmul(sim_ps[:, b, :], wqkT[:, 0:P], gw[:, b, P:2 * P], start=True, stop=True)
            for b in range(NB):
                pe.wait_ge(prod_ready, b + 1)
                t.matmul(norm_ps[:, b * P:(b + 1) * P], ones[:], prod[:, b, P:2 * P], start=True, stop=True)
                last = t.matmul(norm_ps[:, NB * P + b:NB * P + b + 1], prod[:, b, 0:P], ones[:, 0:1],
                                start=True, stop=True)
            last.then_inc(norm_done, 1)

            pe.wait_ge(b1_in, 16)
            pe.wait_ge(tables_ready, 1)
            for c in range(FC):
                last = t.matmul(b1_ps[:, c, :], b1s[:, c * P:(c + 1) * P], of_e[:], start=True, stop=True)
            last.then_inc(b1t_done, 1)
            keep_warm(9, banks[5])

            def middle():
                pe.wait_ge(att_ready, 1)
                for b in range(NB):
                    last = t.matmul(mid_ps[:, b, :], att[:, b, :], woutT[:], start=True, stop=True)
                last.then_inc(mid_done, 1)

            def matrices():
                pe.wait_ge(mid_ready, 1)
                for b in range(NB):
                    last = t.matmul(mat_ps[:, b, :], wqkv[:, 2, :], mid[:, b, :], start=True, stop=True)
                last.then_inc(mat_done, 1)

            def wait_kept(k):
                if 0 <= k < EARLY:
                    pe.wait_ge(xT_early, k + 1)
                elif k >= EARLY:
                    pe.wait_ge(xT_ready, k + 1 - EARLY)

            def transpose_x(k, odd):
                if k in NORM_DVE:
                    pe.wait_ge(xn_dve, NORM_DVE.index(k) + 1)
                else:
                    pe.wait_ge(xn_ready, k + 1 - sum(n < k for n in NORM_DVE))
                wait_kept(k - 2)
                t.transpose(xT_ps[odd][:, 0:P], xns[odd][:], ident[:]).then_inc(xT_done, 1)

            def product1(k, odd):
                wait_kept(k)
                pe.wait_ge(w1_in[k % RING], 16 * (k // RING + 1))
                need(pe, gelu_ready, k - 1)
                for c in range(FC):
                    last = t.matmul(hT_ps[odd][:, c * P:(c + 1) * P], w1r[k % RING][:, c * P:(c + 1) * P],
                                    xTs[k % XT_RING][:], start=True, stop=True)
                last.then_inc(hT_done, 1)

            def attention(k):
                need(pe, s_ready, k - 1)
                t.matmul(s_ps[k % 2][:, 0:NB * P], xTs[k % XT_RING][:], mat[:], start=True, stop=True).then_inc(s_done, 1)

            def product2(k, odd):
                pe.wait_ge(gelu_ready, k + 1)
                need(pe, z_ready, k - 1)
                for c in range(FC):
                    last = t.matmul(y_ps[odd][:, 0:P], gs[odd][:, c * P:(c + 1) * P], w2s[:, bass.ds(w_off[k] + c * P, P)],
                                    start=(c == 0), stop=(c == FC - 1))
                last.then_inc(y_done, 1)

            def turn(i, odd):
                def on(k):
                    return not isinstance(i, int) or 0 <= k < NT
                if on(i + 2):
                    transpose_x(i + 2, odd)
                if on(i + 1):
                    product1(i + 1, 1 - odd)
                for k in attention_of(i):
                    attention(k)
                if on(i - 1):
                    product2(i - 1, 1 - odd)

            pe.wait_ge(tables_ready, 1)
            w_off = offsets(mybir.EngineType.PE, e512_at, (E - 1) * F)
            turn(-2, 0)
            turn(-1, 1)
            product1(1, 1)
            middle()
            matrices()
            transpose_x(2, 0)
            pe.wait_ge(w2_in, 16)
            for i in range(1, NT + 1):
                if i == MAT_TURN:
                    pe.wait_ge(mat_ready, 1)
                turn(i, i % 2)


_INS = ['L0_attn_x', 'L0_attn_norm_weight', 'L0_attn_w_qkv', 'L0_attn_temperature', 'L0_attn_w_out',
        'L0_ffn_Wr', 'L0_ffn_W1', 'L0_ffn_b1', 'L0_ffn_W2', 'L0_ffn_b2']
_OUTS = [((2, 1024, 128), 'float32')]


def kernel(**inputs):
    import numpy as _np
    import concourse.bacc as _bacc
    from concourse import mybir as _mybir
    from concourse.bass_utils import run_bass_kernel_spmd as _run

    nc = _bacc.Bacc("TRN2", target_bir_lowering=False, num_devices=1)
    arrays, args = {}, []
    for name in _INS:
        a = _np.ascontiguousarray(inputs[name])
        arrays[f"in_{name}_dram"] = a
        args.append(nc.dram_tensor(f"in_{name}_dram", a.shape, _mybir.dt.from_np(a.dtype), kind="ExternalInput").ap())
    for i, (shape, dtype) in enumerate(_OUTS):
        dt = _mybir.dt.from_np(_np.dtype(dtype))
        args.append(nc.dram_tensor(f"out_{i}_dram", shape, dt, kind="ExternalOutput").ap())
    build(nc, *args)
    r = _run(nc, [arrays], core_ids=[0])
    got = tuple(r.results[0][f"out_{i}_dram"] for i in range(len(_OUTS)))
    return got[0]
```

```python
from contextlib import ExitStack, nullcontext

import concourse.bass as bass
from concourse import mybir

F32 = mybir.dt.float32
F32R = mybir.dt.float32r
BF16 = mybir.dt.bfloat16
I32 = mybir.dt.int32
ALU = mybir.AluOpType
ACT = mybir.ActivationFunctionType
AX_X = mybir.AxisListType.X
At = bass.IndirectOffsetOnAxis

P = 128
NB = 2
NJ = 16
JB = NJ // NB
T = P * NJ
E = 8
F = 512
FC = F // P
DH = 16
SHIFT = P.bit_length() - 1
NT = T // P + E - 1
SURE = T // P + 1

RING = 4
XT_RING = 6
FLIGHT = 4
EARLY = 2
NORM_DVE = (2, 3, 4)
MAT_TURN = 2
WARM_UP = 5

SHIFTED, RSTD, RA, RB, HALF_P = P, P + 1, P + 2, P + 3, P + 4
ROW = P + 8

LN_EPS = 1e-5
RMS_EPS = 1e-6
NORM_FLOOR = 1e-12
OUTSIDE = 1e30
NOWHERE = 4 * T
SLOTS_POOL = 12
SLOT_CUTS = (0, 5)
BEFORE_RANK = 2


def attention_of(turn):
    return [k for k in range(NT) if max(k + 1, MAT_TURN + k // 2) == turn]


def build(nc, x, norm_w, w_qkv, temperature, w_out, w_r, w1, b1, w2, b2, out):
    x_v = x.rearrange("b (p j) d -> b p j d", p=P)
    out_v = out.rearrange("b n d -> (b n) d")
    rows = nc.dram_tensor("token_rows", (T, ROW), F32).ap()
    rows_v = rows.rearrange("(b p j) r -> b p j r", b=NB, p=P)

    with ExitStack() as ctx:
        def sb(name, shape, dt=F32):
            return ctx.enter_context(nc.sbuf_tensor(name, shape, dt))

        def bank(name):
            return ctx.enter_context(nc.psum_tensor(name, [P, 512], F32))

        def sem(name):
            return ctx.enter_context(nc.semaphore(name))

        ident = sb("ident", [P, P])
        ones = sb("ones", [P, P])
        ones_bf = sb("ones_bf", [P, P], BF16)
        before = sb("before", [P, P], BF16)
        head_gap = sb("head_gap", [P, P])
        head_rows = sb("head_rows", [E, P])
        slot_iota = sb("slot_iota", [P, P], BF16)
        tile_iota = sb("tile_iota", [P, NT], BF16)
        tile_start = sb("tile_start", [P, NT])
        own_e = sb("own_e", [E, 1])
        rev_e = sb("rev_e", [P, E])
        earlier_e = sb("earlier_e", [P, E, E])
        id_p = sb("id_p", [P, NB])
        id_j = sb("id_j", [P, NJ], BF16)
        warm_row = sb("warm_row", [P, F], BF16)
        xe = sb("xe", [P, NJ, ROW])
        wqkv = sb("wqkv", [P, 3, P])
        wout = sb("wout", [P, P])
        nw = sb("nw", [P, 1])
        temp = sb("temp", [E, 1])
        wr = sb("wr", [P, E])
        w2s = sb("w2s", [P, E * F])
        b1s = sb("b1s", [E, F])
        b2s = sb("b2s", [P, E, P])
        stats = sb("stats", [P, NJ, 6])
        mv = sb("mv", [P, NJ, 2])
        v12 = sb("v12", [P, 2, NJ])
        root = sb("root", [P, 2, NJ])
        shift = sb("shift", [P, 2, NJ])
        rs = sb("rs", [P, 2, NJ])
        rt = sb("rt", [P, 2, NJ])
        xr = sb("xr", [P, NJ, P])
        xT = sb("xT", [P, NJ * P])
        wrc = sb("wrc", [P, E])
        lmax = sb("lmax", [P, NJ])
        is_max = sb("is_max", [P, NJ, E])
        best = sb("best", [P, NJ])
        chosen = sb("chosen", [P, NJ + 1, E], BF16)
        below = sb("below", [P, NJ, E])
        expo = sb("expo", [P, NJ, E])
        psum_e = sb("psum_e", [P, NJ])
        p_max = sb("p_max", [P, NJ])
        rfac = sb("rfac", [P, NJ])
        tiles_i = sb("tiles_i", [P, 2, E], I32)
        ee = sb("ee", [P, E, E])
        base = sb("base", [P, E])
        place = sb("place", [P, NJ, E])
        pos_i = sb("pos_i", [P, NJ], I32)
        ab_i = sb("ab_i", [P, 2, NJ], I32)
        ab = sb("ab", [P, 2, NJ], BF16)
        in_tile = sb("in_tile", [P, NJ, NT], BF16)
        tagged = sb("tagged", [P, NJ, 2, NT], BF16)
        in_slot = sb("in_slot", [P, NJ, P], BF16)
        late = sb("late", [P, NT])
        token1 = sb("token1", [P, NT])
        from_row = sb("from_row", [P, NT], I32)
        to_row = sb("to_row", [P, NT], I32)
        et = sb("et", [P, NT, E - 1])
        ef = sb("ef", [P, NT])
        of_e = sb("of_e", [E, NT])
        e128_at = sb("e128_at", [1, NT + 1], I32)
        e512_at = sb("e512_at", [1, NT + 1], I32)
        b1t = sb("b1t", [P, FC, NT])
        wqkT = sb("wqkT", [P, 2 * P])
        woutT = sb("woutT", [P, P])
        gram = sb("gram", [P, NB, P])
        gw = sb("gw", [P, NB, 2 * P])
        prod = sb("prod", [P, NB, 2 * P])
        n2 = sb("n2", [P, NB * P + NB])
        ni = sb("ni", [P, NB * P + NB])
        nt_ = sb("nt_", [P, NB * P + NB])
        etemp = sb("etemp", [P, 1])
        qscale = sb("qscale", [P, NB])
        sim = sb("sim", [P, NB, P])
        smin = sb("smin", [P, NB])
        prob = sb("prob", [P, NB, P])
        psumA = sb("psumA", [P, NB])
        pinv = sb("pinv", [P, NB])
        att = sb("att", [P, NB, P])
        mid = sb("mid", [P, NB, P])
        mat = sb("mat", [P, NB * P])
        mat_hi = sb("mat_hi", [P, NB * P], F32R)
        mat_lo = sb("mat_lo", [P, NB * P], F32R)
        xg = sb("xg", [P, NT, ROW])
        sg = sb("sg", [P, NT, P])
        xns = [sb(f"xns{i}", [P, P]) for i in range(2)]
        xTs = [sb(f"xTs{i}", [P, P]) for i in range(XT_RING)]
        xT_hi = [sb(f"xT_hi{i}", [P, P], F32R) for i in range(RING)]
        xT_lo = [sb(f"xT_lo{i}", [P, P], F32R) for i in range(RING)]
        w1r = [sb(f"w1r{i}", [P, F]) for i in range(RING)]
        gs = [sb(f"gs{i}", [P, F]) for i in range(2)]
        zs = [sb(f"zs{i}", [P, P]) for i in range(2)]
        th = [sb(f"th{i}", [P, P]) for i in range(2)]
        qs = [sb(f"qs{i}", [P, P]) for i in range(RING)]
        us = sb("us", [P, P])

        banks = [bank(f"bank{i}") for i in range(8)]
        hT_ps, xT_ps, y_ps, s_ps = banks[4:6], banks[6:8], (banks[0], banks[3]), banks[1:3]
        logits_ps = banks[4][:, 0:NJ * E].rearrange("p (j e) -> p j e", e=E)
        rank_ps = banks[5][:, 0:(NJ + 1) * E].rearrange("p (j e) -> p j e", e=E)
        wmean_ps, temp_ps = banks[6][:, 0:E], banks[6][:, E:E + 1]
        slots_ps = banks[6][:, 0:2 * NT].rearrange("p (g t) -> p g t", g=2)
        wT_ps = banks[7]
        gram_ps = banks[3][:, 0:NB * P].rearrange("p (b c) -> p b c", b=NB)
        gw_ps = banks[0][:, :].rearrange("p (b c) -> p b c", b=NB)
        sim_ps = banks[1][:, 0:NB * P].rearrange("p (b c) -> p b c", b=NB)
        norm_ps = banks[2][:, 0:NB * P + NB]
        b1_ps = banks[3][:, 0:FC * NT].rearrange("p (c t) -> p c t", c=FC)
        mid_ps = banks[3][:, 0:NB * P].rearrange("p (b c) -> p b c", b=NB)
        mat_ps = banks[2][:, 0:NB * P].rearrange("p (b c) -> p b c", b=NB)

        x_in = [sem(f"x_in{i}") for i in range(NJ // 4)]
        att_w_in = sem("att_w_in")
        wr_in = sem("wr_in")
        w1_in = [sem(f"w1_in{i}") for i in range(RING)]
        w2_in, b1_in, b2_in = sem("w2_in"), sem("b1_in"), sem("b2_in")
        rows_out = sem("rows_out")
        row_in = [sem(f"row_in{i}") for i in range(FLIGHT)]
        result_out = sem("result_out")
        late_result_out = [sem(f"late_result_out{k}") for k in range(SURE, NT)]
        pool_step, dve_step = sem("pool_step"), sem("dve_step")
        warm_ready, ident_ready, const_ready = sem("warm_ready"), sem("ident_ready"), sem("const_ready")
        var_ready, root_ready, rs_ready = sem("var_ready"), sem("root_ready"), sem("rs_ready")
        shift_ready = sem("shift_ready")
        wmean_done, wrc_ready, ln_ready = sem("wmean_done"), sem("wrc_ready"), sem("ln_ready")
        xT_tok_done, xT_tok_ready = sem("xT_tok_done"), sem("xT_tok_ready")
        xr_pool, xr_act = sem("xr_pool"), sem("xr_act")
        logits_done, below_ready, expo_ready = sem("logits_done"), sem("below_ready"), sem("expo_ready")
        chosen_ready, rank_done, tags_ready = sem("chosen_ready"), sem("rank_done"), sem("tags_ready")
        in_slot_ready, in_slot_pool, slots_done = sem("in_slot_ready"), sem("in_slot_pool"), sem("slots_done")
        ab_ready, in_tile_ready, id_tags_ready = sem("ab_ready"), sem("in_tile_ready"), sem("id_tags_ready")
        scalars_ready, from_ready, to_ready, tables_ready = (
            sem("scalars_ready"), sem("from_ready"), sem("to_ready"), sem("tables_ready"))
        b1t_done, b1t_ready = sem("b1t_done"), sem("b1t_ready")
        wT_done, wT_ready, temp_done = sem("wT_done"), sem("wT_ready"), sem("temp_done")
        gram_done, gram_ready, gw_done, gw_ready = sem("gram_done"), sem("gram_ready"), sem("gw_done"), sem("gw_ready")
        prod_pool, prod_dve, norm_done, n2_ready = sem("prod_pool"), sem("prod_dve"), sem("norm_done"), sem("n2_ready")
        nln_ready, nroot_ready, etemp_ready = sem("nln_ready"), sem("nroot_ready"), sem("etemp_ready")
        sim_ready, prob_ready, att_ready = sem("sim_ready"), sem("prob_ready"), sem("att_ready")
        mid_done, mid_ready, mat_done, mat_ready = sem("mid_done"), sem("mid_ready"), sem("mat_done"), sem("mat_ready")
        xn_ready, xT_done, xT_ready = sem("xn_ready"), sem("xT_done"), sem("xT_ready")
        xT_split, mat_split = sem("xT_split"), sem("mat_split")
        xT_early = sem("xT_early")
        xn_dve = sem("xn_dve")
        hT_done, gelu_ready = sem("hT_done"), sem("gelu_ready")
        s_done, s0_ready, s_ready = sem("s_done"), sem("s0_ready"), sem("s_ready")
        y_done, z_ready, tanh_ready = sem("y_done"), sem("z_ready"), sem("tanh_ready")
        q_done, u_done, o_ready = sem("q_done"), sem("u_done"), sem("o_ready")

        def need(eng, semaphore, value):
            if value > 0:
                eng.wait_ge(semaphore, value)

        biases = b2s[:].rearrange("p e d -> p (e d)")
        w1_v = w1.rearrange("e d f -> (e d) f")

        def offsets(engine, table, most):
            return nc.values_load_multi_w_load_instructions(
                table[0:1, :], engines=[engine], min_val=0, max_val=most,
                skip_runtime_bounds_check_because="an expert is 0 to 7 by its construction")[1]

        def count_used(engine):
            return nc.values_load_multi_w_load_instructions(
                e128_at[0:1, NT:NT + 1], engines=[engine], min_val=0, max_val=NT,
                skip_runtime_bounds_check_because="it is 16 to 23 by its construction")[1][0]

        def if_used(eng, used, k):
            return nullcontext() if k < SURE else eng.If(used > k)

        block = ctx.enter_context(nc.Block())

        @block.sync
        def _(sp):
            for i in range(NJ // 4):
                j = i * 4 % JB
                sp.dma_start(xe[:, i * 4:(i + 1) * 4, 0:P], x_v[i * 4 // JB, :, j:j + 4, :]).then_inc(x_in[i], 16)
            sp.dma_start(wqkv[:], w_qkv.rearrange("(s o) c -> o s c", s=3)).then_inc(att_w_in, 16)
            sp.dma_start(wout[:], w_out).then_inc(att_w_in, 16)
            sp.dma_start(w2s[:].rearrange("f (e c d) -> f e c d", e=E, c=FC),
                         w2.rearrange("e (c f) d -> f e c d", c=FC)).then_inc(w2_in, 16)
            sp.dma_start(b1s[:], b1).then_inc(b1_in, 16)
            sp.dma_start(b2s[:], b2.partition_broadcast(P)).then_inc(b2_in, 16)
            sp.wait_ge(scalars_ready, 1)
            for b in range(NB):
                sp.dma_start(rows_v[b], xe[:, b * JB:(b + 1) * JB, :]).then_inc(rows_out, 16)
            sp.wait_ge(tables_ready, 1)
            row_off = offsets(mybir.EngineType.SP, e128_at, (E - 1) * P)
            for k in range(NT):
                with if_used(sp, row_off[NT], k):
                    need(sp, hT_done, k - RING + 1)
                    sp.dma_start(w1r[k % RING][:], w1_v[bass.ds(row_off[k], P), :]).then_inc(w1_in[k % RING], 16)

        @block.gpsimd
        def _(pool):
            steps = [0]

            def link(ins):
                steps[0] += 1
                ins.then_inc(pool_step, 1)
                pool.wait_ge(pool_step, steps[0])

            g = nc.gpsimd
            g.memset(ones_bf[:], 1.0)
            g.memset(warm_row[:], 0.0).then_inc(warm_ready, 1)
            link(g.memset(ones[:], 1.0))
            g.affine_select(out=ident[:], in_=ones[:], compare_op=ALU.is_equal, fill=0.0, base=0,
                            pattern=[[-1, P]], channel_multiplier=1).then_inc(ident_ready, 1)
            g.memset(xe[:, :, SHIFTED:ROW], 0.0)
            g.memset(chosen[:, NJ:NJ + 1, :], 0.0)
            g.affine_select(out=before[:], in_=ones[:], compare_op=ALU.is_gt, fill=0.0, base=0,
                            pattern=[[1, P]], channel_multiplier=-1)
            g.iota(slot_iota[:], [[1, P]], base=0, channel_multiplier=0, allow_small_or_imprecise_dtypes=True)
            g.iota(tile_iota[:], [[1, NT]], base=0, channel_multiplier=0, allow_small_or_imprecise_dtypes=True)
            g.iota(tile_start[:], [[P, NT]], base=0, channel_multiplier=0, allow_small_or_imprecise_dtypes=True)
            g.iota(own_e[:], [[0, 1]], base=0, channel_multiplier=1, allow_small_or_imprecise_dtypes=True)
            g.iota(rev_e[:], [[-1, E]], base=E, channel_multiplier=0, allow_small_or_imprecise_dtypes=True)
            g.iota(id_p[:], [[T // NB, NB]], base=0, channel_multiplier=JB, allow_small_or_imprecise_dtypes=True)
            g.iota(id_j[:], [[0, NB], [1, JB]], base=1, channel_multiplier=0, allow_small_or_imprecise_dtypes=True)
            link(g.memset(earlier_e[:], float(P)))
            g.affine_select(out=earlier_e[:], in_=earlier_e[:], compare_op=ALU.is_gt, fill=0.0, base=0,
                            pattern=[[1, E], [-1, E]], channel_multiplier=0)
            link(g.memset(head_gap[:], 0.0))
            gap = head_gap[:].rearrange("p (h i) -> p h i", i=DH)
            link(g.affine_select(out=gap, in_=gap, compare_op=ALU.is_ge, fill=OUTSIDE, base=0,
                                 pattern=[[-DH, E], [0, DH]], channel_multiplier=1))
            link(g.affine_select(out=gap, in_=gap, compare_op=ALU.is_ge, fill=OUTSIDE, base=DH - 1,
                                 pattern=[[DH, E], [0, DH]], channel_multiplier=-1))
            hr = head_rows[:].rearrange("p (h i) -> p h i", i=DH)
            g.affine_select(out=hr, in_=ones[0:E, :].rearrange("p (h i) -> p h i", i=DH), compare_op=ALU.is_equal,
                            fill=0.0, base=0, pattern=[[-1, E], [0, DH]], channel_multiplier=1
                            ).then_inc(const_ready, 1)

            pool.wait_ge(rs_ready, 1)
            pool.wait_ge(shift_ready, 1)
            for j in range(0, NJ, 2):
                g.tensor_scalar(xr[:, j, :], xe[:, j, 0:P], rs[:, 1, j:j + 1], shift[:, 1, j:j + 1],
                                ALU.mult, ALU.add).then_inc(xr_pool, 1)

            pool.wait_ge(ab_ready, 1)
            for j in range(SLOTS_POOL, NJ):
                g.tensor_scalar(in_slot[:, j, :], slot_iota[:], ab_i[:, 1, j:j + 1], None, ALU.is_equal
                                ).then_inc(in_slot_pool, 1)
            pool.wait_ge(gw_ready, 1)
            g.tensor_tensor(prod[:, 0, :], gw[:, 0, :], wqkT[:], ALU.mult).then_inc(prod_pool, 1)

            pool.wait_ge(rows_out, 16 * NB)
            pool.wait_ge(from_ready, 1)
            for k in range(NT):
                if k >= FLIGHT:
                    pool.wait_ge(row_in[k % FLIGHT], 16 * (k // FLIGHT))
                g.indirect_dma_start(xg[:, k, :], None, rows, At(ap=from_row[:, k:k + 1], axis=0)
                                     ).then_inc(row_in[k % FLIGHT], 16)
            pool.wait_ge(to_ready, 1)
            pool.wait_ge(tables_ready, 1)
            used = count_used(mybir.EngineType.Pool)
            for k in range(NT):
                with if_used(pool, used, k):
                    pool.wait_ge(o_ready, k + 1)
                    g.indirect_dma_start(out_v, At(ap=to_row[:, k:k + 1], axis=0), xg[:, k, 0:P], None,
                                         bounds_check=T - 1, oob_is_err=False
                                         ).then_inc(result_out if k < SURE else late_result_out[k - SURE], 16)
            pool.wait_ge(result_out, 16 * SURE)
            for k in reversed(range(SURE, NT)):
                with if_used(pool, used, k):
                    pool.wait_ge(late_result_out[k - SURE], 16)

        @block.vector
        def _(dve):
            v = nc.vector
            steps = [0]

            def link(ins):
                steps[0] += 1
                ins.then_inc(dve_step, 1)
                dve.wait_ge(dve_step, steps[0])

            def mark(ins):
                steps[0] += 1
                ins.then_inc(dve_step, 1)
                return steps[0]

            def after(count):
                dve.wait_ge(dve_step, count)

            for j in range(NJ):
                if j % 4 == 0:
                    dve.wait_ge(x_in[j // 4], 16)
                if j == 2:
                    dve.wait_ge(wmean_done, 1)
                    v.scalar_tensor_tensor(out=wrc[:], in0=wmean_ps, scalar=-1.0 / P, in1=wr[:],
                                           op0=ALU.mult, op1=ALU.add).then_inc(wrc_ready, 1)
                last = v.bn_stats(stats[:, j, :], xe[:, j, 0:P])
            link(last)
            for j in range(NJ):
                last = v.bn_aggr(mv[:, j, :], stats[:, j, :])
            link(last)
            var = mv[:, :, 1]
            v.tensor_scalar(v12[:, 0, :], var, LN_EPS, None, ALU.add)
            v.tensor_scalar(v12[:, 1, :], var, 1.0 + RMS_EPS, RMS_EPS * LN_EPS, ALU.mult, ALU.add
                            ).then_inc(var_ready, 1)
            dve.wait_ge(var_ready, 1)
            dve.wait_ge(root_ready, 1)
            link(v.scalar_tensor_tensor(out=rt[:], in0=root[:], scalar=-0.5, in1=root[:], op0=ALU.mult, op1=ALU.mult))
            link(v.tensor_tensor(rt[:], rt[:], v12[:], ALU.mult))
            v.scalar_tensor_tensor(out=rs[:], in0=rt[:], scalar=1.5, in1=root[:], op0=ALU.add, op1=ALU.mult
                                   ).then_inc(rs_ready, 1)
            dve.wait_ge(rs_ready, 1)
            v.scalar_tensor_tensor(out=shift[:], in0=mv[:, :, 0].unsqueeze(1).to_broadcast([P, 2, NJ]), scalar=-1.0,
                                   in1=rs[:], op0=ALU.mult, op1=ALU.mult).then_inc(shift_ready, 1)
            dve.wait_ge(const_ready, 1)
            dve.wait_ge(logits_done, 1)
            rev = rev_e[:].unsqueeze(1).to_broadcast([P, NJ, E])
            link(v.tensor_reduce(lmax[:], logits_ps, AX_X, ALU.max))
            max_at = mark(v.tensor_tensor(is_max[:], logits_ps, lmax[:].unsqueeze(2).to_broadcast([P, NJ, E]),
                                          ALU.is_equal))
            rfac_at = mark(v.tensor_tensor(rfac[:], rs[:, 0, :], v12[:, 0, :], ALU.mult))
            after(max_at)
            max_at = mark(v.tensor_tensor(is_max[:], is_max[:], rev, ALU.mult))
            after(rfac_at)
            rfac_at = mark(v.tensor_tensor(rfac[:], rfac[:], rs[:, 1, :], ALU.mult))
            after(max_at)
            link(v.tensor_reduce(best[:], is_max[:], AX_X, ALU.max))
            v.tensor_tensor(chosen[:, 0:NJ, :], rev, best[:].unsqueeze(2).to_broadcast([P, NJ, E]), ALU.is_equal
                            ).then_inc(chosen_ready, 1)
            link(v.tensor_tensor(below[:], logits_ps, lmax[:].unsqueeze(2).to_broadcast([P, NJ, E]), ALU.subtract))
            v.tensor_tensor(below[:], below[:], rs[:, 0, :].unsqueeze(2).to_broadcast([P, NJ, E]), ALU.mult
                            ).then_inc(below_ready, 1)
            dve.wait_ge(shift_ready, 1)
            v.tensor_copy(xe[:, :, SHIFTED], shift[:, 0, :])
            v.tensor_copy(xe[:, :, RSTD], rs[:, 0, :])

            dve.wait_ge(rank_done, 1)
            dve.wait_ge(chosen_ready, 1)
            place_at = mark(v.tensor_scalar(tiles_i[:, 0, :], rank_ps[:, NJ, :], float(P - 1), None, ALU.add))
            dve.wait_ge(expo_ready, 1)
            p_at = mark(v.tensor_reduce(psum_e[:], expo[:], AX_X, ALU.add))
            after(place_at)
            place_at = mark(v.tensor_scalar(tiles_i[:, 1, :], tiles_i[:, 0, :], SHIFT, None, ALU.arith_shift_right))
            after(p_at)
            p_at = mark(v.reciprocal(p_max[:], psum_e[:]))
            after(place_at)
            place_at = mark(v.tensor_tensor(ee[:], earlier_e[:], tiles_i[:, 1, :].unsqueeze(1).to_broadcast([P, E, E]),
                                            ALU.mult))
            after(p_at)
            v.tensor_scalar(xe[:, :, HALF_P], p_max[:], 0.5, None, ALU.mult)
            after(place_at)
            place_at = mark(v.tensor_reduce(base[:], ee[:], AX_X, ALU.add))
            for b, at in enumerate((RA, RB)):
                half = slice(b * JB, (b + 1) * JB)
                last = v.scalar_tensor_tensor(out=xe[:, half, at], in0=p_max[:, half], scalar=0.5, in1=rfac[:, half],
                                              op0=ALU.mult, op1=ALU.mult)
            last.then_inc(scalars_ready, 1)
            after(place_at)
            et_at = mark(v.tensor_tensor(et[:], base[:, 1:E].unsqueeze(1).to_broadcast([P, NT, E - 1]),
                                         tile_start[:].unsqueeze(2).to_broadcast([P, NT, E - 1]), ALU.is_le))
            place_at = mark(v.tensor_tensor(place[:], rank_ps[:, 0:NJ, :],
                                            base[:].unsqueeze(1).to_broadcast([P, NJ, E]), ALU.add))
            after(et_at)
            et_at = mark(v.tensor_reduce(ef[:], et[:], AX_X, ALU.add))
            after(place_at)
            place_at = mark(v.tensor_tensor(place[:], place[:], chosen[:, 0:NJ, :], ALU.mult))
            after(et_at)
            v.tensor_scalar(e128_at[:, 0:NT], ef[0:1, :], float(P), None, ALU.mult)
            after(place_at)
            with nc.allow_low_precision(reason="sums of whole numbers below 2**24, and int32 holds them"):
                place_at = mark(v.tensor_reduce(pos_i[:], place[:], AX_X, ALU.add))
            v.tensor_scalar(e512_at[:, 0:NT], ef[0:1, :], float(F), None, ALU.mult)
            with nc.allow_low_precision(reason="a sum of small whole numbers, and int32 holds it"):
                v.tensor_reduce(e128_at[:, NT:], tiles_i[0:1, 1, :], AX_X, ALU.add)
                v.tensor_reduce(e512_at[:, NT:], tiles_i[0:1, 1, :], AX_X, ALU.add)
            v.tensor_scalar(of_e[:], ef[0:E, :], own_e[:, 0:1], None, ALU.is_equal).then_inc(tables_ready, 1)
            after(place_at)
            v.tensor_scalar(ab_i[:, 0, :], pos_i[:], SHIFT, None, ALU.arith_shift_right)
            link(v.tensor_scalar(ab_i[:, 1, :], pos_i[:], P - 1, None, ALU.bitwise_and))
            v.tensor_copy(ab[:], ab_i[:]).then_inc(ab_ready, 1)
            dve.wait_ge(ab_ready, 1)
            v.tensor_tensor(in_tile[:], ab[:, 0, :].unsqueeze(2).to_broadcast([P, NJ, NT]),
                            tile_iota[:].unsqueeze(1).to_broadcast([P, NJ, NT]), ALU.is_equal
                            ).then_inc(in_tile_ready, 1)
            for lo, hi in zip(SLOT_CUTS, SLOT_CUTS[1:] + (SLOTS_POOL,)):
                v.tensor_tensor(in_slot[:, lo:hi, :], ab[:, 1, lo:hi].unsqueeze(2).to_broadcast([P, hi - lo, P]),
                                slot_iota[:].unsqueeze(1).to_broadcast([P, hi - lo, P]), ALU.is_equal
                                ).then_inc(in_slot_ready, 1)
                if lo == 0:
                    dve.wait_ge(in_tile_ready, 1)
                    v.tensor_tensor(tagged[:, :, 1, :], in_tile[:], id_j[:].unsqueeze(2).to_broadcast([P, NJ, NT]),
                                    ALU.mult).then_inc(tags_ready, 1)
            dve.wait_ge(gw_ready, 1)
            v.tensor_tensor(prod[:, 1, :], gw[:, 1, :], wqkT[:], ALU.mult).then_inc(prod_dve, 1)
            dve.wait_ge(slots_done, 1)
            link(v.tensor_copy(late[:], slots_ps[:, 1, :]))
            link(v.tensor_tensor(token1[:], late[:], slots_ps[:, 0, :], ALU.add))
            v.tensor_scalar(from_row[:], token1[:], -1.0, 0.0, ALU.add, ALU.max).then_inc(from_ready, 1)
            dve.wait_ge(norm_done, 1)
            v.tensor_scalar(n2[:], norm_ps, NORM_FLOOR * NORM_FLOOR, None, ALU.max).then_inc(n2_ready, 1)
            link(v.tensor_scalar(late[:], token1[:], 0.0, float(NOWHERE), ALU.is_equal, ALU.mult))
            link(v.tensor_tensor(token1[:], late[:], token1[:], ALU.add))
            v.tensor_scalar(to_row[:], token1[:], -1.0, None, ALU.add).then_inc(to_ready, 1)
            dve.wait_ge(n2_ready, 1)
            dve.wait_ge(nroot_ready, 1)
            link(v.scalar_tensor_tensor(out=nt_[:], in0=ni[:], scalar=-0.5, in1=ni[:], op0=ALU.mult, op1=ALU.mult))
            link(v.tensor_tensor(nt_[:], nt_[:], n2[:], ALU.mult))
            link(v.scalar_tensor_tensor(out=ni[:], in0=nt_[:], scalar=1.5, in1=ni[:], op0=ALU.add, op1=ALU.mult))
            dve.wait_ge(etemp_ready, 1)
            link(v.tensor_scalar(qscale[:], ni[:, NB * P:], etemp[:, 0:1], -1.0, ALU.mult, ALU.mult))
            for b in range(NB):
                last = v.scalar_tensor_tensor(out=sim[:, b, :], in0=sim_ps[:, b, :], scalar=qscale[:, b:b + 1],
                                              in1=ni[:, b * P:(b + 1) * P], op0=ALU.mult, op1=ALU.mult)
            link(last)
            link(v.tensor_tensor(sim[:], sim[:], head_gap[:].unsqueeze(1).to_broadcast([P, NB, P]), ALU.add))
            v.tensor_reduce(smin[:], sim[:], AX_X, ALU.min).then_inc(sim_ready, 1)
            dve.wait_ge(prob_ready, 1)
            link(v.reciprocal(pinv[:], psumA[:]))
            for b in range(NB):
                last = v.tensor_scalar(att[:, b, :], prob[:, b, :], pinv[:, b:b + 1], None, ALU.mult)
            last.then_inc(att_ready, 1)

            def keep_xT(k):
                dve.wait_ge(xT_done, k + 1)
                need(dve, hT_done, k - XT_RING + 1)
                v.tensor_copy(xTs[k % XT_RING][:], xT_ps[k % 2][:, 0:P]).then_inc(xT_ready, 1)

            def normalise(k):
                dve.wait_ge(row_in[k % FLIGHT], 16 * (k // FLIGHT + 1))
                dve.wait_ge(xT_done, k - 1)
                v.tensor_scalar(xns[k % 2][:], xg[:, k, 0:P], xg[:, k, RSTD:RSTD + 1], xg[:, k, SHIFTED:SHIFTED + 1],
                                ALU.mult, ALU.add).then_inc(xn_dve, 1)

            def split_xT(k):
                if k < EARLY:
                    dve.wait_ge(xT_early, k + 1)
                else:
                    dve.wait_ge(xT_ready, k + 1 - EARLY)
                need(dve, s_done, k - RING + 1)
                kept, hi, lo = xTs[k % XT_RING], xT_hi[k % RING], xT_lo[k % RING]
                link(v.tensor_copy(hi[:], kept[:]))
                v.tensor_tensor(lo[:], kept[:], hi[:], ALU.subtract).then_inc(xT_split, 1)

            def attention(k):
                dve.wait_ge(s0_ready, k + 1)
                row = xg[:, bass.ds(k, 1), :].rearrange("p a r -> p (a r)")
                acc = sg[:, bass.ds(k, 1), :].rearrange("p a r -> p (a r)")
                v.scalar_tensor_tensor(out=acc, in0=s_ps[k % 2][:, P:2 * P], scalar=row[:, RB:RB + 1], in1=acc,
                                       op0=ALU.mult, op1=ALU.add).then_inc(s_ready, 1)

            def ffn_out(k, odd):
                dve.wait_ge(y_done, k + 1)
                v.tensor_tensor(zs[odd][:], y_ps[odd][:, 0:P], biases[:, bass.ds(b_off[k], P)], ALU.add
                                ).then_inc(z_ready, 1)

            def gate(k, odd):
                dve.wait_ge(tanh_ready, k + 1)
                need(dve, u_done, k - RING + 1)
                v.scalar_tensor_tensor(out=qs[k % RING][:], in0=th[odd][:], scalar=1.0, in1=zs[odd][:],
                                       op0=ALU.add, op1=ALU.mult).then_inc(q_done, 1)

            def times_attention(k):
                acc = sg[:, bass.ds(k, 1), :].rearrange("p a r -> p (a r)")
                dve.wait_ge(q_done, k + 1)
                dve.wait_ge(s_ready, k + 1)
                need(dve, o_ready, k)
                v.tensor_tensor(us[:], qs[k % RING][:], acc, ALU.mult).then_inc(u_done, 1)

            def add_x(k):
                row = xg[:, bass.ds(k, 1), :].rearrange("p a r -> p (a r)")
                dve.wait_ge(u_done, k + 1)
                v.tensor_tensor(row[:, 0:P], us[:], row[:, 0:P], ALU.add).then_inc(o_ready, 1)

            def turn(i, odd):
                def on(k):
                    return 0 <= k < NT
                if i + 3 in NORM_DVE:
                    normalise(i + 3)
                if EARLY <= i + 2 < NT:
                    with if_used(dve, used, i + 2):
                        keep_xT(i + 2)
                with if_used(dve, used, i - 2):
                    for k in attention_of(i - 1):
                        attention(k)
                    if on(i - 2):
                        gate(i - 2, odd)
                    for k in attention_of(i - 1):
                        times_attention(k)
                        add_x(k)
                for k in attention_of(i + 1):
                    with if_used(dve, used, k):
                        split_xT(k)
                if on(i - 1):
                    with if_used(dve, used, i - 1):
                        ffn_out(i - 1, 1 - odd)

            dve.wait_ge(b2_in, 16)
            dve.wait_ge(tables_ready, 1)
            b_off = offsets(mybir.EngineType.DVE, e128_at, (E - 1) * P)
            used = b_off[NT]
            normalise(2)
            turn(0, 0)
            dve.wait_ge(mat_ready, 1)
            link(v.tensor_copy(mat_hi[:], mat[:]))
            v.tensor_tensor(mat_lo[:], mat[:], mat_hi[:], ALU.subtract).then_inc(mat_split, 1)
            for i in range(1, NT + 2):
                turn(i, i % 2)

        @block.scalar
        def _(act):
            a = nc.scalar
            act.dma_start(wr[:], w_r).then_inc(wr_in, 16)
            act.dma_start(nw[:], norm_w.rearrange("(c a) -> c a", a=1)).then_inc(att_w_in, 16)
            act.dma_start(temp[:], temperature.rearrange("h a b -> h (a b)")).then_inc(att_w_in, 16)
            a.preload_act_table_set("natural_log_exp_and_others")
            for g4 in range(4):
                act.wait_ge(xT_tok_done, g4 + 1)
                a.activation(xT[:, g4 * F:(g4 + 1) * F], banks[g4][:], ACT.Copy).then_inc(xT_tok_ready, 1)
            act.wait_ge(var_ready, 1)
            a.activation(root[:], v12[:], ACT.Ln).then_inc(ln_ready, 1)
            act.wait_ge(ln_ready, 1)
            a.activation(root[:], root[:], ACT.Exp, scale=-0.5).then_inc(root_ready, 1)
            act.wait_ge(rs_ready, 1)
            act.wait_ge(shift_ready, 1)
            for j in range(1, NJ, 2):
                a.activation(xr[:, j, :], xe[:, j, 0:P], ACT.Identity, bias=shift[:, 1, j:j + 1],
                             scale=rs[:, 1, j:j + 1]).then_inc(xr_act, 1)
                if j == 9:
                    act.wait_ge(below_ready, 1)
                    a.activation(expo[:], below[:], ACT.Exp).then_inc(expo_ready, 1)
            act.wait_ge(wT_done, 1)
            act.wait_ge(att_w_in, 64)
            a.activation(wqkT[:], wT_ps[:, 0:2 * P], ACT.Copy, scale=nw[:, 0:1])
            a.activation(woutT[:], wT_ps[:, 2 * P:3 * P], ACT.Copy).then_inc(wT_ready, 1)
            act.wait_ge(temp_done, 1)
            a.activation(etemp[:], temp_ps, ACT.Exp).then_inc(etemp_ready, 1)
            act.wait_ge(gram_done, 1)
            a.activation(gram[:], gram_ps, ACT.Copy).then_inc(gram_ready, 1)
            act.wait_ge(in_tile_ready, 1)
            for b in range(NB):
                half = slice(b * JB, (b + 1) * JB)
                last = a.activation(tagged[:, half, 0, :], in_tile[:, half, :], ACT.Copy, scale=id_p[:, b:b + 1])
            last.then_inc(id_tags_ready, 1)
            act.wait_ge(gw_done, 1)
            a.activation(gw[:], gw_ps, ACT.Copy).then_inc(gw_ready, 1)
            act.wait_ge(n2_ready, 1)
            a.activation(ni[:], n2[:], ACT.Ln).then_inc(nln_ready, 1)
            act.wait_ge(nln_ready, 1)
            a.activation(ni[:], ni[:], ACT.Exp, scale=-0.5).then_inc(nroot_ready, 1)
            act.wait_ge(b1t_done, 1)
            a.activation(b1t[:], b1_ps, ACT.Copy).then_inc(b1t_ready, 1)

            def normalise(k, odd):
                act.wait_ge(row_in[k % FLIGHT], 16 * (k // FLIGHT + 1))
                need(act, xT_done, k - 1)
                a.activation(xns[odd][:], xg[:, k, 0:P], ACT.Identity, bias=xg[:, k, SHIFTED:SHIFTED + 1],
                             scale=xg[:, k, RSTD:RSTD + 1]).then_inc(xn_ready, 1)

            def attention(k):
                act.wait_ge(s_done, k + 1)
                a.activation(sg[:, bass.ds(k, 1), :].rearrange("p a r -> p (a r)"), s_ps[k % 2][:, 0:P], ACT.Copy,
                             scale=xg[:, bass.ds(k, 1), RA:RA + 1].rearrange("p a r -> p (a r)")
                             ).then_inc(s0_ready, 1)

            def gelu(k, odd, chunks):
                act.wait_ge(hT_done, k + 1)
                need(act, y_done, k - 1)
                for c in chunks:
                    last = a.activation(gs[odd][:, c * P:(c + 1) * P], hT_ps[odd][:, c * P:(c + 1) * P], ACT.Gelu,
                                        bias=b1t[:, c, k:k + 1])
                if c == FC - 1:
                    last.then_inc(gelu_ready, 1)

            def tanh(k, odd):
                act.wait_ge(z_ready, k + 1)
                need(act, q_done, k - 1)
                a.activation(th[odd][:], zs[odd][:], ACT.Tanh,
                             scale=xg[:, bass.ds(k, 1), HALF_P:HALF_P + 1].rearrange("p a r -> p (a r)")
                             ).then_inc(tanh_ready, 1)

            def turn(i, odd):
                def on(k):
                    return 0 <= k < NT
                for k in attention_of(i - 1):
                    with if_used(act, used, k):
                        attention(k)
                if on(i + 3) and i + 3 not in NORM_DVE:
                    with if_used(act, used, i + 3):
                        normalise(i + 3, 1 - odd)
                if on(i):
                    with if_used(act, used, i):
                        gelu(i, odd, range(FC // 2))
                if on(i - 2):
                    with if_used(act, used, i - 2):
                        tanh(i - 2, odd)
                if on(i):
                    with if_used(act, used, i):
                        gelu(i, odd, range(FC // 2, FC))

            def keep_early(k):
                act.wait_ge(xT_done, k + 1)
                a.activation(xTs[k][:], xT_ps[k % 2][:, 0:P], ACT.Copy).then_inc(xT_early, 1)

            act.wait_ge(tables_ready, 1)
            used = count_used(mybir.EngineType.Activation)
            normalise(0, 0)
            normalise(1, 1)
            keep_early(0)
            keep_early(1)
            act.wait_ge(sim_ready, 1)
            for b in range(NB):
                last = a.activation(prob[:, b, :], sim[:, b, :], ACT.Exp, bias=smin[:, b:b + 1], scale=-1.0,
                                    accum_out=psumA[:, b:b + 1])
            last.then_inc(prob_ready, 1)
            a.preload_act_table_set("gelu_and_others")
            act.wait_ge(mid_done, 1)
            a.activation(mid[:], mid_ps, ACT.Copy).then_inc(mid_ready, 1)
            act.wait_ge(b1t_ready, 1)
            turn(0, 0)
            act.wait_ge(mat_done, 1)
            a.activation(mat[:].rearrange("p (b c) -> p b c", b=NB), mat_ps, ACT.Copy, scale=nw[:, 0:1]
                         ).then_inc(mat_ready, 1)
            for i in range(1, NT + 2):
                turn(i, i % 2)

        @block.tensor
        def _(pe):
            t = nc.tensor

            def keep_warm(count, bank):
                for _ in range(count):
                    t.matmul(bank[:], ones_bf[:], warm_row[:], start=True, stop=True)

            pe.wait_ge(warm_ready, 1)
            keep_warm(WARM_UP, banks[7])
            pe.wait_ge(ident_ready, 1)

            def transposes(g4):
                pe.wait_ge(x_in[g4], 16)
                for j in range(g4 * 4, g4 * 4 + 4):
                    last = t.transpose(banks[g4][:, (j % 4) * P:(j % 4 + 1) * P], xe[:, j, 0:P], ident[:])
                last.then_inc(xT_tok_done, 1)

            def logits(g4):
                pe.wait_ge(xT_tok_ready, g4 + 1)
                for j in range(g4 * 4, g4 * 4 + 4):
                    last = t.matmul(logits_ps[:, j, :], xT[:, j * P:(j + 1) * P], wrc[:], start=True, stop=True)
                if g4 == 3:
                    last.then_inc(logits_done, 1)

            transposes(0)
            pe.wait_ge(wr_in, 16)
            t.matmul(wmean_ps, ones[:], wr[:], start=True, stop=True).then_inc(wmean_done, 1)
            transposes(1)
            transposes(2)
            transposes(3)
            pe.wait_ge(wrc_ready, 1)
            for g4 in range(4):
                logits(g4)
            pe.wait_ge(att_w_in, 64)
            t.transpose(wT_ps[:, 0:P], wqkv[:, 0, :], ident[:])
            t.transpose(wT_ps[:, P:2 * P], wqkv[:, 1, :], ident[:])
            t.transpose(wT_ps[:, 2 * P:3 * P], wout[:], ident[:]).then_inc(wT_done, 1)
            pe.wait_ge(const_ready, 1)
            t.matmul(temp_ps, head_rows[:], temp[:], start=True, stop=True).then_inc(temp_done, 1)

            def grams(columns):
                for j in columns:
                    pe.wait_ge(xr_act if j % 2 else xr_pool, j // 2 + 1)
                    last = t.matmul(gram_ps[:, j // JB, :], xr[:, j, :], xr[:, j, :],
                                    start=(j % JB == 0), stop=(j % JB == JB - 1))
                if j == NJ - 1:
                    last.then_inc(gram_done, 1)

            keep_warm(1, banks[0])
            grams(range(BEFORE_RANK))
            pe.wait_ge(chosen_ready, 1)
            t.matmul(rank_ps, before[:], chosen[:], start=True, stop=False, skip_group_check=True)
            for c in range(1, NJ + 1):
                last = t.matmul(rank_ps[:, c:, :], ones_bf[:], chosen[:, 0:NJ + 1 - c, :], start=False,
                                stop=(c == NJ), skip_group_check=True)
            last.then_inc(rank_done, 1)
            grams(range(BEFORE_RANK, NJ))
            pe.wait_ge(wT_ready, 1)
            pe.wait_ge(gram_ready, 1)
            for b in range(NB):
                done = t.matmul(gw_ps[:, b, :], gram[:, b, :], wqkT[:], start=True, stop=True)
            done.then_inc(gw_done, 1)
            pe.wait_ge(etemp_ready, 1)
            pe.wait_ge(tags_ready, 1)
            pe.wait_ge(id_tags_ready, 1)
            for j in range(NJ):
                if j == SLOT_CUTS[1]:
                    pe.wait_ge(gw_ready, 1)
                    for b in range(NB):
                        t.matmul(sim_ps[:, b, :], wqkT[:, 0:P], gw[:, b, P:2 * P], start=True, stop=True)
                if j in SLOT_CUTS:
                    pe.wait_ge(in_slot_ready, SLOT_CUTS.index(j) + 1)
                if j >= SLOTS_POOL:
                    pe.wait_ge(in_slot_pool, j - SLOTS_POOL + 1)
                last = t.matmul(slots_ps, in_slot[:, j, :], tagged[:, j, :, :], start=(j == 0), stop=(j == NJ - 1))
            last.then_inc(slots_done, 1)
            for b in range(NB):
                pe.wait_ge((prod_pool, prod_dve)[b], 1)
                t.matmul(norm_ps[:, b * P:(b + 1) * P], ones[:], prod[:, b, P:2 * P], start=True, stop=True)
                last = t.matmul(norm_ps[:, NB * P + b:NB * P + b + 1], prod[:, b, 0:P], ones[:, 0:1],
                                start=True, stop=True)
            last.then_inc(norm_done, 1)
            pe.wait_ge(b1_in, 16)
            pe.wait_ge(tables_ready, 1)
            for c in range(FC):
                last = t.matmul(b1_ps[:, c, :], b1s[:, c * P:(c + 1) * P], of_e[:], start=True, stop=True)
            last.then_inc(b1t_done, 1)
            keep_warm(9, banks[5])

            def middle():
                pe.wait_ge(att_ready, 1)
                for b in range(NB):
                    last = t.matmul(mid_ps[:, b, :], att[:, b, :], woutT[:], start=True, stop=True)
                last.then_inc(mid_done, 1)

            def matrices():
                pe.wait_ge(mid_ready, 1)
                for b in range(NB):
                    last = t.matmul(mat_ps[:, b, :], wqkv[:, 2, :], mid[:, b, :], start=True, stop=True)
                last.then_inc(mat_done, 1)

            def wait_kept(k):
                if 0 <= k < EARLY:
                    pe.wait_ge(xT_early, k + 1)
                elif k >= EARLY:
                    pe.wait_ge(xT_ready, k + 1 - EARLY)

            def transpose_x(k, odd):
                if k in NORM_DVE:
                    pe.wait_ge(xn_dve, NORM_DVE.index(k) + 1)
                else:
                    pe.wait_ge(xn_ready, k + 1 - sum(n < k for n in NORM_DVE))
                wait_kept(k - 2)
                t.transpose(xT_ps[odd][:, 0:P], xns[odd][:], ident[:]).then_inc(xT_done, 1)

            def product1(k, odd):
                wait_kept(k)
                pe.wait_ge(w1_in[k % RING], 16 * (k // RING + 1))
                need(pe, gelu_ready, k - 1)
                for c in range(FC):
                    last = t.matmul(hT_ps[odd][:, c * P:(c + 1) * P], w1r[k % RING][:, c * P:(c + 1) * P],
                                    xTs[k % XT_RING][:], start=True, stop=True)
                last.then_inc(hT_done, 1)

            def attention(k):
                need(pe, s_ready, k - 1)
                pe.wait_ge(xT_split, k + 1)
                hi, lo = xT_hi[k % RING], xT_lo[k % RING]
                t.matmul(s_ps[k % 2][:, 0:NB * P], hi[:], mat_hi[:], start=True, stop=False)
                t.matmul(s_ps[k % 2][:, 0:NB * P], hi[:], mat_lo[:], start=False, stop=False)
                t.matmul(s_ps[k % 2][:, 0:NB * P], lo[:], mat_hi[:], start=False, stop=True).then_inc(s_done, 1)

            def product2(k, odd):
                pe.wait_ge(gelu_ready, k + 1)
                need(pe, z_ready, k - 1)
                for c in range(FC):
                    last = t.matmul(y_ps[odd][:, 0:P], gs[odd][:, c * P:(c + 1) * P],
                                    w2s[:, bass.ds(w_off[k] + c * P, P)], start=(c == 0), stop=(c == FC - 1))
                last.then_inc(y_done, 1)

            def turn(i, odd):
                def on(k):
                    return 0 <= k < NT
                if on(i + 2):
                    with if_used(pe, used, i + 2):
                        transpose_x(i + 2, odd)
                if on(i + 1):
                    with if_used(pe, used, i + 1):
                        product1(i + 1, 1 - odd)
                with if_used(pe, used, i - 1):
                    for k in attention_of(i):
                        attention(k)
                    if on(i - 1):
                        product2(i - 1, 1 - odd)

            pe.wait_ge(tables_ready, 1)
            w_off = offsets(mybir.EngineType.PE, e512_at, (E - 1) * F)
            used = w_off[NT]
            turn(-2, 0)
            turn(-1, 1)
            product1(1, 1)
            middle()
            matrices()
            transpose_x(2, 0)
            pe.wait_ge(w2_in, 16)
            for i in range(1, NT + 1):
                if i == MAT_TURN:
                    pe.wait_ge(mat_split, 1)
                turn(i, i % 2)


_INS = ['L0_attn_x', 'L0_attn_norm_weight', 'L0_attn_w_qkv', 'L0_attn_temperature', 'L0_attn_w_out',
        'L0_ffn_Wr', 'L0_ffn_W1', 'L0_ffn_b1', 'L0_ffn_W2', 'L0_ffn_b2']
_OUTS = [((2, 1024, 128), 'float32')]


def kernel(**inputs):
    import numpy as _np
    import concourse.bacc as _bacc
    from concourse import mybir as _mybir
    from concourse.bass_utils import run_bass_kernel_spmd as _run

    nc = _bacc.Bacc("TRN2", target_bir_lowering=False, num_devices=1)
    arrays, args = {}, []
    for name in _INS:
        a = _np.ascontiguousarray(inputs[name])
        arrays[f"in_{name}_dram"] = a
        args.append(nc.dram_tensor(f"in_{name}_dram", a.shape, _mybir.dt.from_np(a.dtype), kind="ExternalInput").ap())
    for i, (shape, dtype) in enumerate(_OUTS):
        dt = _mybir.dt.from_np(_np.dtype(dtype))
        args.append(nc.dram_tensor(f"out_{i}_dram", shape, dt, kind="ExternalOutput").ap())
    build(nc, *args)
    r = _run(nc, [arrays], core_ids=[0])
    got = tuple(r.results[0][f"out_{i}_dram"] for i in range(len(_OUTS)))
    return got[0]
```
